# Optimizing a Trainium2 kernel written in Bass

```python
import numpy as np
import jax
import jax.numpy as jnp

def _softmax(x, axis=-1):
    return jax.nn.softmax(x, axis=axis)

def _gelu(x):
    return jax.nn.gelu(x, approximate=True)

def _silu(x):
    return jax.nn.silu(x)

def _sigmoid(x):
    return jax.nn.sigmoid(x)

def _layernorm(x, axis=-1, eps=1e-05):
    m = jnp.mean(x, axis=axis, keepdims=True)
    v = jnp.var(x, axis=axis, keepdims=True)
    return (x - m) / jnp.sqrt(v + eps)

def _scatter_add(tgt, idx, src, axis=0):
    return tgt.at[idx].add(src)

def _segment_sum(src, seg, n):
    return jax.ops.segment_sum(src, seg, n)
kernel_name = 'mk_macaron_d2_jaxref_r4_4fc705'

def setup_inputs(seed: int=0):
    np.random.seed(seed)
    _w = jnp.asarray

    def _L0_attn_setup():
        import jax, jax.numpy as jnp
        import numpy as np
        DIM = 256
        HEADS = 16
        HEAD_DIM = DIM // HEADS
        SCALE = HEAD_DIM ** (-0.5)

        def apply_rope(x, theta=10000.0):
            n, d = (x.shape[2], x.shape[3])
            seq = jnp.arange(n, dtype=jnp.float32)
            inv = 1.0 / theta ** (jnp.arange(0, d, 2, dtype=jnp.float32) / d)
            freqs = seq[:, None] * inv[None, :]
            cos = jnp.cos(freqs)[None, None]
            sin = jnp.sin(freqs)[None, None]
            x1, x2 = jnp.split(x, 2, axis=-1)
            return jnp.concatenate([x1 * cos - x2 * sin, x1 * sin + x2 * cos], axis=-1)
        key = jax.random.key(seed)
        ks = jax.random.split(key, 7)
        s = DIM ** (-0.5)
        return {'x': jax.random.normal(ks[0], (2, 512, DIM), dtype=jnp.float32), 'Wqkv': jax.random.normal(ks[1], (3 * DIM, DIM), dtype=jnp.float32) * s, 'bqkv': jax.random.normal(ks[2], (3 * DIM,), dtype=jnp.float32) * 0.02, 'Wpre': jax.random.normal(ks[3], (HEADS, HEADS), dtype=jnp.float32) * HEADS ** (-0.5), 'Wpost': jax.random.normal(ks[4], (HEADS, HEADS), dtype=jnp.float32) * HEADS ** (-0.5), 'Wout': jax.random.normal(ks[5], (DIM, DIM), dtype=jnp.float32) * s, 'bout': jax.random.normal(ks[6], (DIM,), dtype=jnp.float32) * 0.02}
    _L0_attn_in = _L0_attn_setup()

    def _L0_ffn_setup():
        import jax, jax.numpy as jnp
        import numpy as np
        B, S, H = (4, 512, 256)
        E = 8
        GS = 2
        NG = E // GS
        F = int(H * 4 * (2.0 / 3.0))
        key = jax.random.key(seed)
        ks = jax.random.split(key, 7)
        sc_h = 1.0 / np.sqrt(H)
        sc_f = 1.0 / np.sqrt(F)
        return {'x': jax.random.normal(ks[0], (B, S, H), dtype=jnp.float32), 'Wr': jax.random.normal(ks[1], (H, E), dtype=jnp.float32) * sc_h, 'br': jnp.zeros((E,), dtype=jnp.float32), 'W_up': jax.random.normal(ks[2], (NG, H, F), dtype=jnp.float32) * sc_h, 'b_up': jax.random.normal(ks[3], (NG, F), dtype=jnp.float32) * 0.01, 'W_down': jax.random.normal(ks[4], (E, F, H), dtype=jnp.float32) * sc_f, 'b_down': jax.random.normal(ks[5], (E, H), dtype=jnp.float32) * 0.01}
    _L0_ffn_in = _L0_ffn_setup()

    def _L1_attn_setup():
        import jax, jax.numpy as jnp
        import numpy as np
        DIM = 256
        HEADS = 16
        HEAD_DIM = DIM // HEADS
        FEAT = 64
        B, N = (4, 1024)

        def _elu1(x):
            return jnp.where(x > 0, x + 1.0, jnp.exp(x))
        key = jax.random.key(seed)
        k_x, k_qkv, k_proj, k_wo, k_bo = jax.random.split(key, 5)
        x = jax.random.normal(k_x, (B, N, DIM), dtype=jnp.float32)
        w_qkv = jax.random.normal(k_qkv, (DIM, 3 * DIM), dtype=jnp.float32) * (1.0 / np.sqrt(DIM))
        proj_matrix = jax.random.normal(k_proj, (HEADS, HEAD_DIM, FEAT), dtype=jnp.float32) * (1.0 / np.sqrt(HEAD_DIM))
        w_out = jax.random.normal(k_wo, (DIM, DIM), dtype=jnp.float32) * (1.0 / np.sqrt(DIM))
        b_out = jax.random.normal(k_bo, (DIM,), dtype=jnp.float32) * 0.01
        return {'x': x, 'w_qkv': w_qkv, 'proj_matrix': proj_matrix, 'w_out': w_out, 'b_out': b_out}
    _L1_attn_in = _L1_attn_setup()

    def _L1_ffn_setup():
        import jax, jax.numpy as jnp
        import numpy as np
        DIM = 256

        def _reference_tuple_inner(x, W_r, W_k, W_v, mu_r, mu_k):
            B, T, C = x.shape
            x_prev = jnp.concatenate([jnp.zeros((B, 1, C), x.dtype), x[:, :-1, :]], axis=1)
            xr = mu_r * x + (1.0 - mu_r) * x_prev
            xk = mu_k * x + (1.0 - mu_k) * x_prev
            r = jax.nn.sigmoid(jnp.einsum('btc,dc->btd', xr, W_r))
            k = jnp.einsum('btc,dc->btd', xk, W_k)
            k_act = jnp.square(jax.nn.relu(k))
            out = r * jnp.einsum('btc,dc->btd', k_act, W_v)
            new_state = x[:, -1, :]
            return (out, new_state)
        key = jax.random.key(seed)
        ks = jax.random.split(key, 6)
        B, T, C = (8, 512, DIM)
        x = jax.random.normal(ks[0], (B, T, C), dtype=jnp.float32)
        s = 1.0 / np.sqrt(C)
        W_r = jax.random.uniform(ks[1], (C, C), jnp.float32, -s, s)
        W_k = jax.random.uniform(ks[2], (C, C), jnp.float32, -s, s)
        W_v = jax.random.uniform(ks[3], (C, C), jnp.float32, -s, s)
        mu_r = jax.random.uniform(ks[4], (C,), jnp.float32)
        mu_k = jax.random.uniform(ks[5], (C,), jnp.float32)
        return {'x': x, 'W_r': W_r, 'W_k': W_k, 'W_v': W_v, 'mu_r': mu_r, 'mu_k': mu_k}
    _L1_ffn_in = _L1_ffn_setup()
    _d = {'L0_attn_x': _L0_attn_in['x'], 'L0_attn_Wqkv': _L0_attn_in['Wqkv'], 'L0_attn_bqkv': _L0_attn_in['bqkv'], 'L0_attn_Wpre': _L0_attn_in['Wpre'], 'L0_attn_Wpost': _L0_attn_in['Wpost'], 'L0_attn_Wout': _L0_attn_in['Wout'], 'L0_attn_bout': _L0_attn_in['bout'], 'L0_ffn_Wr': _L0_ffn_in['Wr'], 'L0_ffn_br': _L0_ffn_in['br'], 'L0_ffn_W_up': _L0_ffn_in['W_up'], 'L0_ffn_b_up': _L0_ffn_in['b_up'], 'L0_ffn_W_down': _L0_ffn_in['W_down'], 'L0_ffn_b_down': _L0_ffn_in['b_down'], 'L1_attn_w_qkv': _L1_attn_in['w_qkv'], 'L1_attn_proj_matrix': _L1_attn_in['proj_matrix'], 'L1_attn_w_out': _L1_attn_in['w_out'], 'L1_attn_b_out': _L1_attn_in['b_out'], 'L1_ffn_W_r': _L1_ffn_in['W_r'], 'L1_ffn_W_k': _L1_ffn_in['W_k'], 'L1_ffn_W_v': _L1_ffn_in['W_v'], 'L1_ffn_mu_r': _L1_ffn_in['mu_r'], 'L1_ffn_mu_k': _L1_ffn_in['mu_k']}
    _x0 = _d['L0_attn_x']
    _d['L0_attn_x'] = jax.random.normal(jax.random.fold_in(jax.random.key(seed), 1), (4, 1024, 256), dtype=_x0.dtype)
    del _x0
    return _d

def reference(L0_attn_x, L0_attn_Wqkv, L0_attn_bqkv, L0_attn_Wpre, L0_attn_Wpost, L0_attn_Wout, L0_attn_bout, L0_ffn_Wr, L0_ffn_br, L0_ffn_W_up, L0_ffn_b_up, L0_ffn_W_down, L0_ffn_b_down, L1_attn_w_qkv, L1_attn_proj_matrix, L1_attn_w_out, L1_attn_b_out, L1_ffn_W_r, L1_ffn_W_k, L1_ffn_W_v, L1_ffn_mu_r, L1_ffn_mu_k):

    def _L0_attn_ref(x, Wqkv, bqkv, Wpre, Wpost, Wout, bout):
        import jax, jax.numpy as jnp
        import numpy as np
        DIM = 256
        HEADS = 16
        HEAD_DIM = DIM // HEADS
        SCALE = HEAD_DIM ** (-0.5)

        def apply_rope(x, theta=10000.0):
            n, d = (x.shape[2], x.shape[3])
            seq = jnp.arange(n, dtype=jnp.float32)
            inv = 1.0 / theta ** (jnp.arange(0, d, 2, dtype=jnp.float32) / d)
            freqs = seq[:, None] * inv[None, :]
            cos = jnp.cos(freqs)[None, None]
            sin = jnp.sin(freqs)[None, None]
            x1, x2 = jnp.split(x, 2, axis=-1)
            return jnp.concatenate([x1 * cos - x2 * sin, x1 * sin + x2 * cos], axis=-1)
        b, n, _ = x.shape
        qkv = x @ Wqkv.T + bqkv
        q, k, v = jnp.split(qkv, 3, axis=-1)
        reshape = lambda t: t.reshape(b, n, HEADS, HEAD_DIM).transpose(0, 2, 1, 3)
        q, k, v = (reshape(q), reshape(k), reshape(v))
        q = apply_rope(q)
        k = apply_rope(k)
        logits = jnp.einsum('bhid,bhjd->bhij', q, k) * SCALE
        logits = jnp.einsum('bhij,gh->bgij', logits, Wpre)
        attn = jax.nn.softmax(logits, axis=-1)
        attn = jnp.einsum('bhij,gh->bgij', attn, Wpost)
        out = jnp.einsum('bhij,bhjd->bhid', attn, v)
        out = out.transpose(0, 2, 1, 3).reshape(b, n, DIM)
        return out @ Wout.T + bout

    def _L0_ffn_ref(x, Wr, br, W_up, b_up, W_down, b_down):
        import jax, jax.numpy as jnp
        import numpy as np
        B, S, H = (4, 512, 256)
        E = 8
        GS = 2
        NG = E // GS
        F = int(H * 4 * (2.0 / 3.0))
        b, s, h = x.shape
        n_tok = b * s
        k = n_tok // E
        xf = x.reshape(n_tok, h)
        logits = xf @ Wr + br
        Sm = jax.nn.softmax(logits, axis=-1)
        G_t, idx_t = jax.lax.top_k(Sm.T, k)
        G = G_t.T
        idx = idx_t.T
        tokens = xf[idx]
        group = jnp.arange(E) // GS
        Wu = W_up[group]
        bu = b_up[group]
        mid = jax.nn.silu(jnp.einsum('keh,ehf->kef', tokens, Wu) + bu)
        out = jnp.einsum('kef,efh->keh', mid, W_down) + b_down
        y = jnp.zeros_like(xf).at[idx].add(G[..., None] * out)
        return y.reshape(b, s, h)

    def _L1_attn_ref(x, w_qkv, proj_matrix, w_out, b_out):
        import jax, jax.numpy as jnp
        import numpy as np
        DIM = 256
        HEADS = 16
        HEAD_DIM = DIM // HEADS
        FEAT = 64
        B, N = (4, 1024)

        def _elu1(x):
            return jnp.where(x > 0, x + 1.0, jnp.exp(x))
        b, n, d = x.shape
        h, hd = (HEADS, HEAD_DIM)
        qkv = x @ w_qkv
        q, k, v = jnp.split(qkv, 3, axis=-1)
        to_heads = lambda t: t.reshape(b, n, h, hd).transpose(0, 2, 1, 3)
        q, k, v = (to_heads(q), to_heads(k), to_heads(v))
        q_proj = _elu1(jnp.einsum('bhnd,hdf->bhnf', q, proj_matrix))
        k_proj = _elu1(jnp.einsum('bhnd,hdf->bhnf', k, proj_matrix))
        kv = jnp.einsum('bhnf,bhnd->bhfd', k_proj, v)
        attn = jnp.einsum('bhnf,bhfd->bhnd', q_proj, kv)
        k_sum = k_proj.sum(axis=2)
        z = 1.0 / (jnp.einsum('bhnf,bhf->bhn', q_proj, k_sum) + 1e-08)
        attn = attn * z[..., None]
        out = attn.transpose(0, 2, 1, 3).reshape(b, n, d)
        return out @ w_out + b_out

    def _L1_ffn_ref(x, W_r, W_k, W_v, mu_r, mu_k):
        import jax, jax.numpy as jnp
        import numpy as np
        DIM = 256

        def _reference_tuple_inner(x, W_r, W_k, W_v, mu_r, mu_k):
            B, T, C = x.shape
            x_prev = jnp.concatenate([jnp.zeros((B, 1, C), x.dtype), x[:, :-1, :]], axis=1)
            xr = mu_r * x + (1.0 - mu_r) * x_prev
            xk = mu_k * x + (1.0 - mu_k) * x_prev
            r = jax.nn.sigmoid(jnp.einsum('btc,dc->btd', xr, W_r))
            k = jnp.einsum('btc,dc->btd', xk, W_k)
            k_act = jnp.square(jax.nn.relu(k))
            out = r * jnp.einsum('btc,dc->btd', k_act, W_v)
            new_state = x[:, -1, :]
            return (out, new_state)
        return _reference_tuple_inner(x, W_r, W_k, W_v, mu_r, mu_k)[0]
    x = L0_attn_x
    x = x + 0.5 * _L0_ffn_ref(_layernorm(x, axis=-1), L0_ffn_Wr, L0_ffn_br, L0_ffn_W_up, L0_ffn_b_up, L0_ffn_W_down, L0_ffn_b_down)
    x = x + _L0_attn_ref(_layernorm(x, axis=-1), L0_attn_Wqkv, L0_attn_bqkv, L0_attn_Wpre, L0_attn_Wpost, L0_attn_Wout, L0_attn_bout)
    x = x + 0.5 * _L0_ffn_ref(_layernorm(x, axis=-1), L0_ffn_Wr, L0_ffn_br, L0_ffn_W_up, L0_ffn_b_up, L0_ffn_W_down, L0_ffn_b_down)
    x = x + 0.5 * _L1_ffn_ref(_layernorm(x, axis=-1), L1_ffn_W_r, L1_ffn_W_k, L1_ffn_W_v, L1_ffn_mu_r, L1_ffn_mu_k)
    x = x + _L1_attn_ref(_layernorm(x, axis=-1), L1_attn_w_qkv, L1_attn_proj_matrix, L1_attn_w_out, L1_attn_b_out)
    x = x + 0.5 * _L1_ffn_ref(_layernorm(x, axis=-1), L1_ffn_W_r, L1_ffn_W_k, L1_ffn_W_v, L1_ffn_mu_r, L1_ffn_mu_k)
    return x

_drawn_inputs = setup_inputs


def setup_inputs(seed=0):
    import zlib

    import numpy as np

    out = dict(_drawn_inputs(seed))
    spreads = {'L0_ffn_br': (0.0, 0.1)}
    factors = {'L0_ffn_b_up': 22.25,
     'L0_ffn_b_down': 8.0,
     'L1_attn_proj_matrix': 27.894,
     'L1_attn_b_out': 6.055,
     'L1_ffn_W_r': 3.282,
     'L1_ffn_mu_r': 6.617}
    for name, (base, spread) in spreads.items():
        noise = np.random.default_rng([zlib.crc32(name.encode()), seed]).standard_normal(out[name].shape)
        drawn = base * np.exp(spread * noise) if base else spread * noise
        out[name] = jnp.asarray(drawn.astype(out[name].dtype))
    for name, factor in factors.items():
        out[name] = (out[name] * factor).astype(out[name].dtype)
    return out
```

```python
import math
from contextlib import ExitStack, contextmanager

import concourse.bass as bass
from concourse import mybir

P = 128
ALU = mybir.AluOpType
ACT = mybir.ActivationFunctionType
F32 = mybir.dt.float32
BF16 = mybir.dt.bfloat16
I32 = mybir.dt.int32
AX_X = mybir.AxisListType.X

BATCH, SEQ, DIM = 4, 1024, 256
KC = DIM // P
TILES = BATCH * SEQ // P
CHUNK = 512
CT = CHUNK // P
CHUNKS = BATCH * SEQ // CHUNK
LN_EPS = 1e-5


class Common:
    pass


def chain(engine, sem):
    count = [0]

    def link(instruction):
        count[0] += 1
        instruction.then_inc(sem, 1)
        engine.wait_ge(sem, count[0])

    return link


@contextmanager
def stage_semaphores(nc, name):
    taken = []

    def sem(n):
        taken.append(nc.alloc_semaphore(name=f"{name}_{n}"))
        return taken[-1]

    yield sem
    nc.clear_and_free_semaphores(taken)
    nc.all_engine_barrier()


def layernorm_stats(nc, g, name):
    with ExitStack() as ctx:
        sem = ctx.enter_context(stage_semaphores(nc, name))
        variance_ready = sem("variance_ready")
        stats_ready = sem("stats_ready")
        aggr_ready = sem("aggr_ready")
        block = ctx.enter_context(nc.Block())

        @block.vector
        def _(dve):
            for t in range(TILES):
                nc.vector.bn_stats(g.stats[:, t, :], g.x[:, t, :]).then_inc(stats_ready, 1)
            dve.wait_ge(stats_ready, TILES)
            for t in range(TILES):
                nc.vector.bn_aggr(g.aggr[:, t, :], g.stats[:, t, :]).then_inc(aggr_ready, 1)
            dve.wait_ge(aggr_ready, TILES)
            nc.vector.tensor_scalar(g.var_eps[:, :], g.aggr[:, :, 1], LN_EPS, None, ALU.add).then_inc(variance_ready, 1)

        @block.gpsimd
        def _(pool):
            pool.wait_ge(variance_ready, 1)
            nc.gpsimd.tensor_tensor(g.rstd[:, :], g.var_eps[:, :], g.minus_half[:, :], ALU.pow)


@contextmanager
def residual(nc, g, name):
    with ExitStack() as ctx:
        sb = lambda n, s, d=F32: ctx.enter_context(nc.sbuf_tensor(n, s, d))
        g.x = sb(f"{name}_x_residual", [P, TILES, DIM])
        g.stats = sb(f"{name}_ln_stats", [P, TILES, 6])
        g.aggr = sb(f"{name}_ln_aggr", [P, TILES, 2])
        g.var_eps = sb(f"{name}_ln_var_eps", [P, TILES])
        g.rstd = sb(f"{name}_ln_rstd", [P, TILES])
        g.minus_half = sb(f"{name}_minus_half", [P, TILES])
        yield


def copy_in(nc, g, name, x_dram, x_in, ident_in):
    with ExitStack() as ctx:
        sem = ctx.enter_context(stage_semaphores(nc, name))
        loaded = sem("copied")
        block = ctx.enter_context(nc.Block())

        @block.sync
        def _(sp):
            sp.dma_start(x_dram, x_in).then_inc(loaded, 16)
            sp.dma_start(g.ident[:, :], ident_in).then_inc(loaded, 16)
            sp.wait_ge(loaded, 32)


def setup(nc, g, name, x_in):
    with ExitStack() as ctx:
        sem = ctx.enter_context(stage_semaphores(nc, name))
        loaded = sem("x_loaded")
        block = ctx.enter_context(nc.Block())

        @block.sync
        def _(sp):
            for b in range(BATCH):
                per = TILES // BATCH
                sp.dma_start(g.x[:, b * per:(b + 1) * per, :],
                             x_in[b * SEQ:(b + 1) * SEQ, :].rearrange("(t p) d -> p t d", p=P)).then_inc(loaded, 16)
            sp.wait_ge(loaded, 16 * BATCH)

        @block.vector
        def _(dve):
            nc.vector.memset(g.minus_half[:, :], -0.5)


def store(nc, g, out):
    with ExitStack() as ctx:
        sem = ctx.enter_context(stage_semaphores(nc, "out"))
        stored = sem("x_stored")
        block = ctx.enter_context(nc.Block())

        @block.sync
        def _(sp):
            per = TILES // BATCH
            for b in range(BATCH):
                sp.dma_start(out[b * SEQ:(b + 1) * SEQ, :].rearrange("(t p) d -> p t d", p=P),
                             g.x[:, b * per:(b + 1) * per, :]).then_inc(stored, 16)
            sp.wait_ge(stored, 16 * BATCH)


def channel_mix(nc, g, name, w_r, w_k, w_v, mu_r, mu_k):
    layernorm_stats(nc, g, f"{name}_ln")
    with ExitStack() as ctx:
        sb = lambda n, s, d=F32: ctx.enter_context(nc.sbuf_tensor(f"{name}_{n}", s, d))
        ps = lambda n, s: ctx.enter_context(nc.psum_tensor(f"{name}_{n}", s, F32))
        sem = ctx.enter_context(stage_semaphores(nc, name))
        w = sb("w", [P, 3, KC, DIM])
        mu = sb("mu", [P, 2, KC])
        xn = sb("xn", [P, CT, DIM])
        xT = sb("xT", [P, KC, CHUNK + 1])
        diff = sb("diff", [P, KC, CHUNK])
        xr = sb("xr", [P, KC, CHUNK])
        xk = sb("xk", [P, KC, CHUNK])
        gate = sb("gate", [P, CT, DIM])
        krelu = sb("krelu", [P, KC, CHUNK])
        kact = sb("kact", [P, KC, CHUNK])
        delta = sb("delta", [P, CT, DIM])
        psT = ps("psT", [P, KC, CHUNK])
        psR = ps("psR", [P, CT, DIM])
        psK = ps("psK", [P, KC, CHUNK])
        psV = ps("psV", [P, CT, DIM])

        weights_in = sem("weights_in")
        chunk_open = sem("chunk_open")
        xn_ready = sem("xn_ready")
        transposed = sem("transposed")
        xT_ready = sem("xT_ready")
        edge_ready = sem("edge_ready")
        diff_ready = sem("diff_ready")
        mixed_ready = sem("mixed_ready")
        r_done = sem("r_done")
        k_done = sem("k_done")
        krelu_ready = sem("krelu_ready")
        kact_ready = sem("kact_ready")
        gate_ready = sem("gate_ready")
        v_done = sem("v_done")
        delta_ready = sem("delta_ready")
        block = ctx.enter_context(nc.Block())

        @block.sync
        def _(sp):
            for n, wt in enumerate((w_r, w_k, w_v)):
                sp.dma_start(w[:, n], wt.rearrange("(c p) d -> p c d", p=P)).then_inc(weights_in, 16)
            for n, m in enumerate((mu_r, mu_k)):
                sp.dma_start(mu[:, n, :], m).then_inc(weights_in, 16)
            sp.wait_ge(weights_in, 16 * 5)

        @block.vector
        def _(dve):
            dve.sem_inc(chunk_open, 1)
            dve.wait_ge(weights_in, 16 * 5)
            with dve.Fori(0, CHUNKS // 2) as i:
                for half in range(2):
                    n = i * 2 + half
                    for t in range(CT):
                        tile = n * CT + t
                        last = nc.vector.tensor_scalar(
                            xn[:, t, :], g.x[:, bass.ds(tile, 1), :].rearrange("p a d -> p (a d)"),
                            g.aggr[:, bass.ds(tile, 1), 0], g.rstd[:, bass.ds(tile, 1)], ALU.subtract, ALU.mult)
                    last.then_inc(xn_ready, 1)
                    if half == 0:
                        nc.vector.memset(xT[:, :, 0:1], 0.0).then_inc(edge_ready, 1)
                    else:
                        nc.vector.tensor_copy(xT[:, :, 0:1], xT[:, :, CHUNK:CHUNK + 1]).then_inc(edge_ready, 1)
                    dve.wait_ge(edge_ready, n + 1)
                    dve.wait_ge(xT_ready, n + 1)
                    nc.vector.tensor_tensor(diff[:, :, :], xT[:, :, 1:CHUNK + 1], xT[:, :, 0:CHUNK], ALU.subtract).then_inc(diff_ready, 1)
                    dve.wait_ge(diff_ready, n + 1)
                    for m, mixed in enumerate((xr, xk)):
                        for c in range(KC):
                            last = nc.vector.scalar_tensor_tensor(
                                mixed[:, c, :], diff[:, c, :], mu[:, m, c:c + 1], xT[:, c, 0:CHUNK], ALU.mult, ALU.add)
                    last.then_inc(mixed_ready, 1)
                    dve.wait_ge(gate_ready, n + 1)
                    dve.wait_ge(v_done, n + 1)
                    nc.vector.scalar_tensor_tensor(delta[:, :, :], psV[:, :, :], 0.5, gate[:, :, :], ALU.mult, ALU.mult).then_inc(delta_ready, 1)
                    dve.wait_ge(delta_ready, n + 1)
                    xs = g.x[:, bass.ds(n * CT, CT), :]
                    nc.vector.tensor_tensor(xs, xs, delta[:, :, :], ALU.add).then_inc(chunk_open, 1)

        @block.tensor
        def _(pe):
            pe.wait_ge(weights_in, 16 * 5)
            with pe.Fori(0, CHUNKS) as n:
                pe.wait_ge(xn_ready, n + 1)
                for t in range(CT):
                    for c in range(KC):
                        last = nc.tensor.transpose(psT[:, c, t * P:(t + 1) * P], xn[:, t, c * P:(c + 1) * P], g.ident[:, :])
                last.then_inc(transposed, 1)
                pe.wait_ge(mixed_ready, n + 1)
                for t in range(CT):
                    for c in range(KC):
                        last = nc.tensor.matmul(psR[:, t, :], xr[:, c, t * P:(t + 1) * P], w[:, 0, c, :], start=c == 0, stop=c == KC - 1)
                last.then_inc(r_done, 1)
                for d in range(KC):
                    for c in range(KC):
                        last = nc.tensor.matmul(psK[:, d, :], w[:, 1, c, d * P:(d + 1) * P], xk[:, c, :], start=c == 0, stop=c == KC - 1)
                last.then_inc(k_done, 1)
                pe.wait_ge(kact_ready, n + 1)
                for t in range(CT):
                    for c in range(KC):
                        last = nc.tensor.matmul(psV[:, t, :], kact[:, c, t * P:(t + 1) * P], w[:, 2, c, :], start=c == 0, stop=c == KC - 1)
                last.then_inc(v_done, 1)

        @block.scalar
        def _(act):
            with act.Fori(0, CHUNKS) as n:
                act.wait_ge(edge_ready, n + 1)
                act.wait_ge(transposed, n + 1)
                nc.scalar.copy(xT[:, :, 1:CHUNK + 1], psT[:, :, :]).then_inc(xT_ready, 1)
                act.wait_ge(r_done, n + 1)
                nc.scalar.activation(gate[:, :, :], psR[:, :, :], ACT.Sigmoid).then_inc(gate_ready, 1)
                act.wait_ge(k_done, n + 1)
                nc.scalar.activation(krelu[:, :, :], psK[:, :, :], ACT.Relu).then_inc(krelu_ready, 1)

        @block.gpsimd
        def _(pool):
            with pool.Fori(0, CHUNKS) as n:
                pool.wait_ge(krelu_ready, n + 1)
                nc.gpsimd.tensor_tensor(kact[:, :, :], krelu[:, :, :], krelu[:, :, :], ALU.mult).then_inc(kact_ready, 1)


HEADS = 16
HD = DIM // HEADS
HALF = HD // 2
SCALE = HD ** -0.5
BT = SEQ // P
GI = P // HEADS
GROUPS = SEQ // GI
TG = P // GI
SLOTS = 4
OC = HEADS // 4
P_SCALE = 4096.0
A_MAX = 16384.0
V_MAX = 16384.0
F16 = mybir.dt.float16
F32R = mybir.dt.float32r


def talking_heads(nc, g, x_dram, w_qkv, b_qkv, w_pre, w_post, w_post_all, w_out, b_out, cos, sin, same_token):
    with ExitStack() as ctx:
        sb = lambda n, s, d=F32: ctx.enter_context(nc.sbuf_tensor(f"at_{n}", s, d))
        ps = lambda n, s: ctx.enter_context(nc.psum_tensor(f"at_{n}", s, F32))
        sem = ctx.enter_context(stage_semaphores(nc, "at"))
        x = sb("x", [P, BT, DIM])
        wqkv = sb("wqkv", [P, KC, 3 * DIM])
        wout = sb("wout", [P, OC, DIM])
        bqkv = sb("bqkv", [P, 3 * DIM])
        bout = sb("bout", [P, DIM])
        cost = sb("cos", [P, BT, HALF])
        sint = sb("sin", [P, BT, HALF])
        wpre = sb("wpre", [P, KC, HEADS])
        wpost16 = sb("wpost16", [P, HEADS])
        samet = sb("same_token", [P, P])
        wpost = sb("wpost", [P, HEADS, GI])
        xn = sb("xn", [P, BT, DIM])
        xnT = sb("xnT", [P, 2, KC, P])
        stats = sb("stats", [P, BT, 6])
        aggr = sb("aggr", [P, BT, 2])
        var_eps = sb("var_eps", [P, BT])
        rstd = sb("rstd", [P, BT])
        minus_half = sb("minus_half", [P, BT])
        qkv = sb("qkv", [P, 3 * DIM])
        rope_a = sb("rope_a", [P, 2 * HEADS, 2, HALF])
        rot = sb("rot", [P, 2 * HEADS, 2, HALF])
        qT = sb("qT", [P, KC, SEQ])
        k_hi = sb("k_hi", [P, KC, SEQ], F32R)
        k_lo = sb("k_lo", [P, KC, SEQ], F32R)
        k_bf = sb("k_bf", [P, KC, SEQ], BF16)
        v_parts = sb("v_parts", [P, BT, HEADS, 2, HD], F16)
        ones = sb("ones", [P, P])
        wsquare = sb("wsquare", [P, KC, DIM])
        vmax = sb("vmax", [P, 4])
        q_full = sb("q_full", [P, KC, HEADS, GI])
        q_hi = sb("q_hi", [P, SLOTS, KC, HEADS * GI], F32R)
        q_lo = sb("q_lo", [P, SLOTS, KC, HEADS * GI], BF16)
        nmax = sb("nmax", [P, SLOTS])
        nbias = sb("nbias", [P, SLOTS])
        psum_row = sb("prob_sum", [P, SLOTS])
        rsum = sb("rsum", [P, SLOTS])
        wp_hi = sb("wp_hi", [P, SLOTS, P], F16)
        wp_lo = sb("wp_lo", [P, SLOTS, P], F16)
        p_full = sb("p_full", [P, SLOTS, SEQ])
        p_hi = sb("p_hi", [P, SLOTS, SEQ], F16)
        p_lo = sb("p_lo", [P, SLOTS, SEQ], F16)
        a_hi = sb("a_hi", [P, BT, HEADS, P], F16)
        a_lo = sb("a_lo", [P, BT, HEADS, P], F16)
        oT = sb("oT", [P, BT, OC, P])
        wabs = sb("wabs", [P, HEADS * HEADS])
        wmax = sb("wmax", [P, 1])
        unscale = sb("unscale", [P, 1])
        rescale = sb("rescale", [P, 1])

        psL = ps("logits", [P, 2, SEQ])
        psM = ps("mixed", [P, 2, 512])
        psO = ps("o", [P, OC, P])
        psT = ps("misc", [P, 512])

        const_in = sem("const_in")
        const_ready = sem("const_ready")
        norms_done = sem("norms_done")
        norm_ready = sem("norm_ready")
        root_ready = sem("root_ready")
        x_in = sem("x_in")
        x_out = sem("x_out")
        stats_ready = sem("stats_ready")
        stats_waited = sem("stats_waited")
        aggr_ready = sem("aggr_ready")
        var_ready = sem("var_ready")
        rstd_ready = sem("rstd_ready")
        xn_ready = sem("xn_ready")
        xn_transposed = sem("xn_transposed")
        xnT_ready = sem("xnT_ready")
        qkv_done = sem("qkv_done")
        qkv_ready = sem("qkv_ready")
        v_waited = sem("v_waited")
        v_part = sem("v_part")
        v_ready = sem("v_ready")
        rope_ready = sem("rope_ready")
        rot_ready = sem("rot_ready")
        rot_read = sem("rot_read")
        rot_transposed = sem("rot_transposed")
        qk_copied = sem("qk_copied")
        qk_ready = sem("qk_ready")
        q_full_done = sem("q_full_done")
        q_hi_done = sem("q_hi_done")
        q_built = sem("q_built")
        logits_done = sem("logits_done")
        max_done = sem("max_done")
        bias_done = sem("bias_done")
        exp_done = sem("exp_done")
        rsum_done = sem("rsum_done")
        wp_part = sem("wp_part")
        wp_ready = sem("wp_ready")
        p_hi_done = sem("p_hi_done")
        p_lo_done = sem("p_lo_done")
        mixed_done = sem("mixed_done")
        a_hi_done = sem("a_hi_done")
        a_lo_done = sem("a_lo_done")
        o_done = sem("o_done")
        oT_ready = sem("oT_ready")
        out_done = sem("out_done")
        biased = sem("biased")
        x_ready = sem("x_ready")
        block = ctx.enter_context(nc.Block())

        made = lambda n: n + 1 + SLOTS
        free = lambda n: n + 1
        made2 = lambda n: n + 1 + 2
        free2 = lambda n: n + 1
        CONSTS = 11

        def groups(eng, b, step):
            def quad(t, q, left=SLOTS, after_tile=False):
                for slot in range(SLOTS):
                    step(b, t, q * SLOTS + slot, slot, min(left + SLOTS - 1 - slot, SLOTS), after_tile and slot == 0)

            quads = TG // SLOTS
            quad(0, 0)
            with eng.Fori(1, quads) as q:
                quad(0, q)
            with eng.Fori(1, BT - 1) as t:
                quad(t, 0, after_tile=True)
                with eng.Fori(1, quads) as q:
                    quad(t, q)
            quad(BT - 1, 0, after_tile=True)
            with eng.Fori(1, quads - 1) as q:
                quad(BT - 1, q)
            quad(BT - 1, quads - 1, left=0)

        @block.sync
        def _(sp):
            bc = lambda a: a.partition_broadcast(P)
            for dst, src in ((wqkv[:, :, :], w_qkv.rearrange("(c p) d -> p c d", p=P)),
                             (wout[:, :, :], w_out),
                             (bqkv[:, :], bc(b_qkv)), (bout[:, :], bc(b_out)),
                             (cost[:, :, :], cos.rearrange("(t p) f -> p t f", p=P)),
                             (sint[:, :, :], sin.rearrange("(t p) f -> p t f", p=P)),
                             (wpre[:, 0, :], w_pre[0:P, :]), (wpre[:, 1, :], w_pre[P:DIM, :]),
                             (wpost16[:, :], w_post), (samet[:, :], same_token),
                             (wabs[:, :], bc(w_post_all))):
                sp.dma_start(dst, src).then_inc(const_in, 16)
            for b in range(BATCH):
                rows = x_dram[bass.ds(b * SEQ, SEQ), :].rearrange("(t p) d -> p t d", p=P)
                sp.dma_start(x[:, :, :], rows).then_inc(x_in, 16)
                sp.wait_ge(x_ready, (b + 1) * BT)
                sp.dma_start(rows, x[:, :, :]).then_inc(x_out, 16)
                sp.wait_ge(x_out, (b + 1) * 16)

        @block.vector
        def _(dve):
            for sem_ in (q_hi_done, max_done, bias_done, rsum_done, wp_part, wp_ready):
                dve.sem_inc(sem_, SLOTS)
            dve.sem_inc(a_lo_done, 2)
            dve.sem_inc(rot_read, 1)
            nc.vector.memset(minus_half[:, :], -0.5).then_inc(const_ready, 1)
            dve.wait_ge(const_in, 16 * CONSTS)
            nc.vector.tensor_scalar(wpre[:, :, :], wpre[:, :, :], SCALE, None, ALU.mult).then_inc(const_ready, 1)
            nc.vector.tensor_tensor(wpost[:, :, :], wpost16[:, :].unsqueeze(2).broadcast_to([P, HEADS, GI]),
                                    samet[:, :].rearrange("p (g i) -> p g i", i=GI), ALU.mult).then_inc(const_ready, 1)
            nc.vector.memset(ones[:, :], 1.0).then_inc(const_ready, 1)
            nc.vector.memset(vmax[:, 3:4], 0.5).then_inc(const_ready, 1)
            nc.vector.tensor_reduce(wmax[:, :], wabs[:, :], AX_X, ALU.max, apply_absolute_value=True).then_inc(const_ready, 1)
            nc.vector.tensor_tensor(wsquare[:, :, :], wqkv[:, :, 2 * DIM:], wqkv[:, :, 2 * DIM:], ALU.mult).then_inc(const_ready, 1)
            nc.vector.tensor_reduce(vmax[:, 1:2], bqkv[:, 2 * DIM:], AX_X, ALU.max, apply_absolute_value=True).then_inc(const_ready, 1)
            dve.wait_ge(const_ready, 8)
            nc.vector.tensor_scalar(unscale[:, :], wmax[:, :], HEADS / A_MAX, 1e-30, ALU.mult, ALU.max).then_inc(const_ready, 1)
            dve.wait_ge(const_ready, 9)
            nc.vector.reciprocal(rescale[:, :], unscale[:, :]).then_inc(const_ready, 1)
            dve.wait_ge(const_ready, 10)
            nc.vector.tensor_scalar(wpost[:, :, :], wpost[:, :, :], rescale[:, 0:1], P_SCALE, ALU.mult, ALU.mult).then_inc(const_ready, 1)
            dve.wait_ge(norms_done, 1)
            nc.vector.tensor_reduce(vmax[:, 0:1], psM[:, 0, 0:DIM], AX_X, ALU.max).then_inc(norm_ready, 1)
            dve.wait_ge(root_ready, 1)
            nc.vector.tensor_scalar(vmax[:, 2:3], vmax[:, 2:3], DIM ** 0.5, vmax[:, 1:2], ALU.mult, ALU.add).then_inc(norm_ready, 1)
            dve.wait_ge(norm_ready, 2)
            nc.vector.tensor_scalar(vmax[:, 2:3], vmax[:, 2:3], 1 / V_MAX, 1e-30, ALU.mult, ALU.max).then_inc(norm_ready, 1)
            dve.wait_ge(norm_ready, 3)
            nc.vector.reciprocal(vmax[:, 0:1], vmax[:, 2:3]).then_inc(norm_ready, 1)
            nc.vector.tensor_tensor(unscale[:, :], unscale[:, :], vmax[:, 2:3], ALU.mult).then_inc(norm_ready, 1)
            dve.wait_ge(norm_ready, 5)
            nc.vector.tensor_scalar(wqkv[:, :, 2 * DIM:], wqkv[:, :, 2 * DIM:], vmax[:, 0:1], None, ALU.mult).then_inc(norm_ready, 1)
            nc.vector.tensor_scalar(bqkv[:, 2 * DIM:], bqkv[:, 2 * DIM:], vmax[:, 0:1], None, ALU.mult).then_inc(norm_ready, 1)
            dve.wait_ge(norm_ready, 7)

            def high_q(b, k, slot):
                src = qT[:, :, bass.ds(k * GI, GI)].unsqueeze(2).broadcast_to([P, KC, HEADS, GI])
                weights = wpre[:, :, :].unsqueeze(3).broadcast_to([P, KC, HEADS, GI])
                dve.wait_ge(logits_done, free(b * GROUPS + k))
                nc.vector.tensor_tensor(q_hi[:, slot].rearrange("p c (g i) -> p c g i", i=GI), src, weights, ALU.mult).then_inc(q_hi_done, 1)

            def row_max(n, slot):
                dve.wait_ge(logits_done, made(n))
                nc.vector.tensor_reduce(nmax[:, slot:slot + 1], psL[:, slot % 2, :], AX_X, ALU.max, negate=True).then_inc(max_done, 1)
                dve.wait_ge(max_done, made(n))
                nc.vector.tensor_scalar(nbias[:, slot:slot + 1], nmax[:, slot:slot + 1], math.log(P_SCALE), None, ALU.add).then_inc(bias_done, 1)

            def post_weights(n, slot):
                dve.wait_ge(exp_done, made(n))
                nc.vector.reciprocal(rsum[:, slot:slot + 1], psum_row[:, slot:slot + 1]).then_inc(rsum_done, 1)
                dve.wait_ge(rsum_done, made(n))
                dve.wait_ge(mixed_done, free(n) * 2)
                flat = wpost[:, :, :].rearrange("p g i -> p (g i)")
                nc.vector.tensor_scalar(wp_hi[:, slot, :], flat, rsum[:, slot:slot + 1], None, ALU.mult).then_inc(wp_part, 1)
                dve.wait_ge(wp_part, made(n))
                nc.vector.scalar_tensor_tensor(wp_lo[:, slot, :], flat, rsum[:, slot:slot + 1],
                                               wp_hi[:, slot, :], ALU.mult, ALU.subtract).then_inc(wp_ready, 1)

            def step(b, t, k, slot, left, after_tile):
                n = b * GROUPS + t * TG + k
                ahead = (slot + 2) % SLOTS
                if left >= 2:
                    row_max(n + 2, ahead)
                for half in range(2):
                    h = n * 2 + half
                    dve.wait_ge(a_hi_done, made2(h))
                    blocks = slice(half * 4, half * 4 + 4)
                    nc.vector.scalar_tensor_tensor(
                        a_lo[:, blocks, :, bass.ds(k * GI, GI)].rearrange("p j g i -> p (j g) i"),
                        psM[:, half, :].rearrange("p (j i) -> p j i", i=GI), 1 / P_SCALE,
                        a_hi[:, blocks, :, bass.ds(k * GI, GI)].rearrange("p j g i -> p (j g) i"),
                        ALU.mult, ALU.subtract).then_inc(a_lo_done, 1)
                if left >= SLOTS:
                    high_q(b, t * TG + k + SLOTS, slot)
                if left >= 2:
                    post_weights(n + 2, ahead)

            with dve.Fori(0, BATCH) as b:
                dve.wait_ge(x_in, (b + 1) * 16)
                for t in range(BT):
                    nc.vector.bn_stats(stats[:, t, :], x[:, t, :]).then_inc(stats_ready, 1)
                dve.wait_ge(stats_ready, (b + 1) * BT)
                dve.sem_inc(stats_waited, 1)
                for t in range(BT):
                    nc.vector.bn_aggr(aggr[:, t, :], stats[:, t, :]).then_inc(aggr_ready, 1)
                dve.wait_ge(aggr_ready, (b + 1) * BT)
                nc.vector.tensor_scalar(var_eps[:, :], aggr[:, :, 1], LN_EPS, None, ALU.add).then_inc(var_ready, 1)
                dve.wait_ge(rstd_ready, b + 1)
                for t in range(BT):
                    nc.vector.tensor_scalar(xn[:, t, :], x[:, t, :], aggr[:, t, 0:1], rstd[:, t:t + 1],
                                            ALU.subtract, ALU.mult).then_inc(xn_ready, 1)

                def k_low(t):
                    m = b * BT + t
                    dve.wait_ge(qk_copied, m + 1)
                    cols = slice(t * P, (t + 1) * P)
                    nc.vector.tensor_tensor(k_lo[:, :, cols], psT[:, 256:512].rearrange("p (c i) -> p c i", c=KC),
                                            k_hi[:, :, cols].bitcast(F32), ALU.subtract).then_inc(qk_ready, 1)

                for t in range(BT):
                    m = b * BT + t
                    dve.wait_ge(qkv_done, m + 1)
                    dve.wait_ge(v_ready, m + 1)
                    dve.wait_ge(rot_read, m + 1)
                    nc.vector.tensor_tensor(qkv[:, :], psL[:, t % 2, 0:3 * DIM], bqkv[:, :], ALU.add).then_inc(qkv_ready, 1)
                    dve.wait_ge(qkv_ready, m + 1)
                    qk = qkv[:, 0:2 * DIM].rearrange("p (h a f) -> p h a f", a=2, f=HALF)
                    c1 = cost[:, t, :].unsqueeze(1).broadcast_to([P, 2 * HEADS, HALF])
                    s1 = sint[:, t, :].unsqueeze(1).broadcast_to([P, 2 * HEADS, HALF])
                    nc.vector.tensor_tensor(rope_a[:, :, 0, :], qk[:, :, 1, :], s1, ALU.mult).then_inc(rope_ready, 1)
                    nc.vector.tensor_tensor(rope_a[:, :, 1, :], qk[:, :, 0, :], s1, ALU.mult).then_inc(rope_ready, 1)
                    dve.wait_ge(rot_transposed, m + 1)
                    nc.vector.tensor_tensor(rot[:, :, 0, :], qk[:, :, 0, :], c1, ALU.mult).then_inc(rope_ready, 1)
                    nc.vector.tensor_tensor(rot[:, :, 1, :], qk[:, :, 1, :], c1, ALU.mult).then_inc(rope_ready, 1)
                    dve.wait_ge(rope_ready, (m + 1) * 4)
                    nc.vector.tensor_tensor(rot[:, :, 0, :], rot[:, :, 0, :], rope_a[:, :, 0, :], ALU.subtract).then_inc(rot_ready, 1)
                    nc.vector.tensor_tensor(rot[:, :, 1, :], rot[:, :, 1, :], rope_a[:, :, 1, :], ALU.add).then_inc(rot_ready, 1)
                    dve.wait_ge(rot_ready, (m + 1) * 2)
                    dve.sem_inc(rot_read, 1)
                    if t:
                        k_low(t - 1)
                k_low(BT - 1)

                for k in range(SLOTS):
                    high_q(b, k, k)
                for slot in range(2):
                    row_max(b * GROUPS + slot, slot)
                    post_weights(b * GROUPS + slot, slot)
                groups(dve, b, step)
                for t in range(BT):
                    m = b * BT + t
                    nc.vector.tensor_tensor(x[:, t, :], x[:, t, :], bout[:, :], ALU.add).then_inc(biased, 1)
                    dve.wait_ge(biased, m + 1)
                    dve.wait_ge(out_done, m + 1)
                    nc.vector.tensor_tensor(x[:, t, :], x[:, t, :], psL[:, t % 2, 0:DIM], ALU.add).then_inc(x_ready, 1)

        @block.gpsimd
        def _(pool):
            for sem_ in (q_built, p_lo_done):
                pool.sem_inc(sem_, SLOTS)
            pool.sem_inc(v_ready, 1)
            pool.wait_ge(const_ready, 11)
            pool.wait_ge(norm_ready, 1)
            nc.gpsimd.tensor_tensor(vmax[:, 2:3], vmax[:, 0:1], vmax[:, 3:4], ALU.pow).then_inc(root_ready, 1)
            weights = wpre[:, :, :].unsqueeze(3).broadcast_to([P, KC, HEADS, GI])

            def build_q(b, k, slot):
                n = b * GROUPS + k
                src = qT[:, :, bass.ds(k * GI, GI)].unsqueeze(2).broadcast_to([P, KC, HEADS, GI])
                pool.wait_ge(q_built, n + SLOTS)
                nc.gpsimd.tensor_tensor(q_full[:, :, :, :], src, weights, ALU.mult).then_inc(q_full_done, 1)
                pool.wait_ge(q_full_done, n + 1)
                pool.wait_ge(q_hi_done, made(n))
                nc.gpsimd.tensor_tensor(q_lo[:, slot], q_full[:, :, :, :].rearrange("p c g i -> p c (g i)"),
                                        q_hi[:, slot].bitcast(F32), ALU.subtract).then_inc(q_built, 1)

            def low_p(n, slot):
                pool.wait_ge(p_hi_done, made(n))
                nc.gpsimd.tensor_tensor(p_lo[:, slot, :], p_full[:, slot, :], p_hi[:, slot, :], ALU.subtract).then_inc(p_lo_done, 1)

            def step(b, t, k, slot, left, after_tile):
                low_p(b * GROUPS + t * TG + k, slot)
                if left >= SLOTS - 1:
                    build_q(b, t * TG + k + SLOTS - 1, (slot - 1) % SLOTS)

            with pool.Fori(0, BATCH) as b:
                pool.wait_ge(var_ready, b + 1)
                nc.gpsimd.tensor_tensor(rstd[:, :], var_eps[:, :], minus_half[:, :], ALU.pow).then_inc(rstd_ready, 1)
                for t in range(BT):
                    m = b * BT + t
                    v = qkv[:, 2 * DIM:3 * DIM].rearrange("p (h f) -> p h f", f=HD)
                    pool.wait_ge(qkv_ready, m + 1)
                    pool.sem_inc(v_waited, 1)
                    nc.gpsimd.tensor_copy(v_parts[:, t, :, 0, :], v).then_inc(v_part, 1)
                    pool.wait_ge(v_part, m + 1)
                    nc.gpsimd.tensor_tensor(v_parts[:, t, :, 1, :], v, v_parts[:, t, :, 0, :], ALU.subtract).then_inc(v_ready, 1)
                pool.wait_ge(qk_ready, (b + 1) * BT)
                for k in range(SLOTS - 1):
                    build_q(b, k, k)
                groups(pool, b, step)

        @block.scalar
        def _(act):
            for sem_ in (exp_done, p_hi_done):
                act.sem_inc(sem_, SLOTS)
            act.sem_inc(a_hi_done, 2)
            act.sem_inc(oT_ready, 1)

            def softmax_exp(n, slot):
                act.wait_ge(bias_done, made(n))
                act.wait_ge(p_lo_done, free(n))
                act.wait_ge(rsum_done, free(n))
                nc.scalar.activation(p_full[:, slot, :], psL[:, slot % 2, :], ACT.Exp, bias=nbias[:, slot:slot + 1],
                                     accum_out=psum_row[:, slot:slot + 1]).then_inc(exp_done, 1)

            def high_p(n, slot):
                act.wait_ge(exp_done, made(n))
                act.wait_ge(mixed_done, free(n) * 2)
                nc.scalar.copy(p_hi[:, slot, :], p_full[:, slot, :]).then_inc(p_hi_done, 1)

            def high_a(n, k, half):
                act.wait_ge(mixed_done, n * 2 + half + 1 + 2 * SLOTS)
                nc.scalar.mul(a_hi[:, half * 4:half * 4 + 4, :, bass.ds(k * GI, GI)],
                              psM[:, half, :].rearrange("p (j g i) -> p j g i", j=4, g=HEADS), 1 / P_SCALE).then_inc(a_hi_done, 1)

            def copy_o(b, t):
                act.wait_ge(o_done, b * BT + t + 1)
                nc.scalar.activation(oT[:, bass.ds(t, 1), :, :].rearrange("p a c i -> p (a c i)"),
                                     psO[:, :, :].rearrange("p c i -> p (c i)"), ACT.Copy, scale=unscale[:, 0:1]).then_inc(oT_ready, 1)

            def step(b, t, k, slot, left, after_tile):
                n = b * GROUPS + t * TG + k
                high_a(n, k, 0)
                high_a(n, k, 1)
                if left >= 2:
                    softmax_exp(n + 2, (slot + 2) % SLOTS)
                    high_p(n + 2, (slot + 2) % SLOTS)
                if after_tile:
                    copy_o(b, t - 1)

            act.wait_ge(norm_ready, 7)
            with act.Fori(0, BATCH) as b:
                def qk_copy(t):
                    m = b * BT + t
                    act.wait_ge(rot_transposed, m + 2)
                    cols = slice(t * P, (t + 1) * P)
                    nc.scalar.copy(qT[:, :, cols], psT[:, 0:256].rearrange("p (c i) -> p c i", c=KC))
                    kps = psT[:, 256:512].rearrange("p (c i) -> p c i", c=KC)
                    nc.scalar.copy(k_bf[:, :, cols], kps)
                    nc.scalar.copy(k_hi[:, :, cols], kps).then_inc(qk_copied, 1)

                for t in range(BT):
                    m = b * BT + t
                    act.wait_ge(xn_transposed, m + 1)
                    nc.scalar.copy(xnT[:, t % 2], psM[:, t % 2, 0:DIM].rearrange("p (c i) -> p c i", c=KC)).then_inc(xnT_ready, 1)
                    if t:
                        qk_copy(t - 1)
                qk_copy(BT - 1)
                for slot in range(2):
                    softmax_exp(b * GROUPS + slot, slot)
                    high_p(b * GROUPS + slot, slot)
                groups(act, b, step)
                copy_o(b, BT - 1)

        @block.tensor
        def _(pe):
            pe.sem_inc(logits_done, SLOTS)
            pe.sem_inc(mixed_done, 2 * SLOTS)
            pe.sem_inc(rot_transposed, 1)
            pe.wait_ge(const_ready, 8)
            for c in range(KC):
                last = nc.tensor.matmul(psM[:, 0, 0:DIM], ones[:, :], wsquare[:, c, :], start=c == 0, stop=c == KC - 1)
            last.then_inc(norms_done, 1)
            pe.wait_ge(norm_ready, 7)

            def logits(n, slot):
                pe.wait_ge(q_built, made(n))
                pe.wait_ge(exp_done, n - 1 + SLOTS)
                for half in range(2):
                    keys = slice(half * 512, half * 512 + 512)
                    k = 0
                    for c in range(KC):
                        for left, right in ((q_hi, k_hi), (q_hi, k_lo), (q_lo, k_bf)):
                            last = nc.tensor.matmul(psL[:, slot % 2, keys], left[:, slot, c, :], right[:, c, keys], start=k == 0, stop=k == 5)
                            k += 1
                last.then_inc(logits_done, 1)

            def mix(n, slot):
                pe.wait_ge(wp_ready, made(n))
                pe.wait_ge(p_lo_done, made(n))
                for half in range(2):
                    pe.wait_ge(a_lo_done, free2(n * 2 + half))
                    for j in range(4):
                        keys = slice(half * 512 + j * P, half * 512 + (j + 1) * P)
                        out = psM[:, half, j * P:(j + 1) * P]
                        nc.tensor.matmul(out, p_hi[:, slot, keys], wp_hi[:, slot, :], start=True, stop=False)
                        nc.tensor.matmul(out, p_hi[:, slot, keys], wp_lo[:, slot, :], start=False, stop=False)
                        last = nc.tensor.matmul(out, p_lo[:, slot, keys], wp_hi[:, slot, :], start=False, stop=True)
                    last.then_inc(mixed_done, 1)

            def attend(b, t):
                m = b * BT + t
                pe.wait_ge(a_lo_done, made2((m + 1) * TG * 2 - 1))
                pe.wait_ge(oT_ready, m + 1)
                for c in range(OC):
                    for j in range(BT):
                        for k, a in enumerate((a_hi, a_lo)):
                            for q in range(4):
                                h = c * 4 + q
                                last = nc.tensor.matmul(psO[q * 32:(q + 1) * 32, c, :], v_parts[:, j, h].rearrange("p s f -> p (s f)"), a[:, j, h, :],
                                                        start=j == 0 and k == 0, stop=j == BT - 1 and k == 1, skip_group_check=True)
                last.then_inc(o_done, 1)

            def step(b, t, k, slot, left, after_tile):
                n = b * GROUPS + t * TG + k
                if left >= 2:
                    logits(n + 2, (slot + 2) % SLOTS)
                if after_tile:
                    attend(b, t - 1)
                mix(n, slot)

            with pe.Fori(0, BATCH) as b:
                def qk_transpose(t):
                    m = b * BT + t
                    pe.wait_ge(rot_ready, (m + 1) * 2)
                    if t:
                        pe.wait_ge(qk_ready, m)
                    else:
                        pe.wait_ge(xn_ready, b * BT + 1)
                    flat = rot[:, :, :, :].rearrange("p h a f -> p (h a f)")
                    for c in range(2 * KC):
                        last = nc.tensor.transpose(psT[:, c * P:(c + 1) * P], flat[:, c * P:(c + 1) * P], g.ident[:, :])
                    last.then_inc(rot_transposed, 1)

                for t in range(BT):
                    m = b * BT + t
                    pe.wait_ge(xn_ready, m + 1)
                    if t >= 2:
                        pe.wait_ge(xnT_ready, m - 1)
                    for c in range(KC):
                        last = nc.tensor.transpose(psM[:, t % 2, c * P:(c + 1) * P], xn[:, t, c * P:(c + 1) * P], g.ident[:, :])
                    last.then_inc(xn_transposed, 1)
                    pe.wait_ge(xnT_ready, m + 1)
                    if t >= 2:
                        pe.wait_ge(qkv_ready, m - 1)
                    for lo, hi in ((0, 512), (512, 768)):
                        for c in range(KC):
                            last = nc.tensor.matmul(psL[:, t % 2, lo:hi], xnT[:, t % 2, c, :], wqkv[:, c, lo:hi], start=c == 0, stop=c == KC - 1)
                    last.then_inc(qkv_done, 1)
                    if t:
                        qk_transpose(t - 1)
                qk_transpose(BT - 1)
                pe.wait_ge(qk_ready, (b + 1) * BT)
                pe.wait_ge(v_ready, (b + 1) * BT + 1)
                for slot in range(2):
                    logits(b * GROUPS + slot, slot)
                groups(pe, b, step)
                attend(b, BT - 1)
                for t in range(BT):
                    m = b * BT + t
                    pe.wait_ge(oT_ready, m + 2)
                    if t >= 2:
                        pe.wait_ge(x_ready, m - 1)
                    for c in range(OC):
                        last = nc.tensor.matmul(psL[:, t % 2, 0:DIM], oT[:, t, c, :], wout[:, c, :], start=c == 0, stop=c == OC - 1)
                    last.then_inc(out_done, 1)


FEAT = 64
PAIRS = HEADS // 2
V1 = HD + 1
HPC = P // HD
Z_EPS = 1e-8


def linear_attention(nc, g, name, w_qkv, proj, w_out, b_out):
    layernorm_stats(nc, g, f"{name}_ln")
    with ExitStack() as ctx:
        sb = lambda n, s, d=F32: ctx.enter_context(nc.sbuf_tensor(f"{name}_{n}", s, d))
        ps = lambda n, s: ctx.enter_context(nc.psum_tensor(f"{name}_{n}", s, F32))
        sem = ctx.enter_context(stage_semaphores(nc, name))
        HB = SEQ // CHUNK
        wqkv = sb("wqkv", [P, KC, 3 * DIM])
        wout = sb("wout", [P, KC, DIM])
        bout = sb("bout", [P, DIM])
        proj_diag = sb("proj_diag", [P, KC, HPC * FEAT])
        xn = sb("xn", [P, BT, DIM])
        xT = sb("xT", [P, KC, CHUNK])
        qT = sb("qT", [P, KC, SEQ])
        kT = sb("kT", [P, KC, SEQ])
        v_one = sb("v_one", [P, BT, HEADS, V1])
        negative = sb("negative", [P, 2, CHUNK])
        exped = sb("exped", [P, 2, CHUNK])
        k_feat = sb("k_feat", [P, BT, HEADS * FEAT])
        q_feat = sb("q_feat", [P, PAIRS, SEQ])
        kv = sb("kv", [P, PAIRS, 2 * V1])
        z = sb("z", [P, HEADS])
        o = sb("o", [P, 2, DIM])
        oT = sb("oT", [P, 2, KC, P])
        delta = sb("delta", [P, 2, DIM])
        psT = ps("psT", [P, KC, CHUNK])
        psQ = ps("psQ", [P, 2, CHUNK])
        psF = ps("psF", [P, 2, CHUNK])
        psKV = ps("psKV", [P, PAIRS, 2 * V1])
        psO = ps("psO", [P, PAIRS, 2 * V1])

        const_in = sem("const_in")
        diag_zero = sem("diag_zero")
        diag_in = sem("diag_in")
        ones_set = sem("ones_set")
        xn_ready = sem("xn_ready")
        transposed = sem("transposed")
        psT_free = sem("psT_free")
        xT_ready = sem("xT_ready")
        proj_done = sem("proj_done")
        out_done = sem("out_done")
        slot_free = [sem(f"slot_free{s}") for s in range(2)]
        qkv_ready = sem("qkv_ready")
        feat_done = sem("feat_done")
        psF_free = sem("psF_free")
        negative_ready = sem("negative_ready")
        exp_ready = sem("exp_ready")
        kv_done = sem("kv_done")
        kv_ready = sem("kv_ready")
        attended = sem("attended")
        z_sum = sem("z_sum")
        z_ready = sem("z_ready")
        o_ready = sem("o_ready")
        o_transposed = sem("o_transposed")
        oT_ready = sem("oT_ready")
        delta_ready = sem("delta_ready")
        delta_free = sem("delta_free")
        block = ctx.enter_context(nc.Block())
        K_UNITS = BT * KC
        UNITS = K_UNITS + HB * PAIRS
        QKV_UNITS = HB * 6
        SLOT_USES = (QKV_UNITS + BT) // 2
        T_USES = HB + BT

        @block.sync
        def _(sp):
            sp.dma_start(wqkv[:, :, :], w_qkv.rearrange("(c p) d -> p c d", p=P)).then_inc(const_in, 16)
            sp.dma_start(wout[:, :, :], w_out.rearrange("(c p) d -> p c d", p=P)).then_inc(const_in, 16)
            sp.dma_start(bout[:, :], b_out.partition_broadcast(P)).then_inc(const_in, 16)
            sp.wait_ge(diag_zero, 1)
            for h in range(HEADS):
                c, m = h // HPC, h % HPC
                sp.dma_start(proj_diag[m * HD:(m + 1) * HD, c, m * FEAT:(m + 1) * FEAT], proj[h]).then_inc(diag_in, 16)

        @block.vector
        def _(dve):
            def less_than_zero(b, u):
                dve.wait_ge(feat_done, b * UNITS + (u + 1))
                nc.vector.tensor_scalar(negative[:, u % 2, :], psF[:, u % 2, :], 0.0, None, ALU.min).then_inc(negative_ready, 1)

            def feature(b, u):
                if u < K_UNITS:
                    into = k_feat[:, u // KC, (u % KC) * CHUNK:(u % KC + 1) * CHUNK]
                else:
                    h, pair = divmod(u - K_UNITS, PAIRS)
                    into = q_feat[:, pair, h * CHUNK:(h + 1) * CHUNK]
                dve.wait_ge(exp_ready, b * UNITS + (u + 1))
                nc.vector.scalar_tensor_tensor(into, psF[:, u % 2, :], 0.0, exped[:, u % 2, :], ALU.max, ALU.add).then_inc(psF_free, 1)

            def normalise(b, t):
                n = b * BT + t
                dve.wait_ge(attended, n + 1)
                heads = psO[:, :, :].rearrange("p a (m v) -> p (a m) v", v=V1)
                nc.vector.tensor_scalar(z[:, :], heads[:, :, HD], Z_EPS, None, ALU.add).then_inc(z_sum, 1)
                dve.wait_ge(z_sum, n + 1)
                nc.vector.reciprocal(z[:, :], z[:, :]).then_inc(z_ready, 1)
                dve.wait_ge(z_ready, n + 1)
                nc.vector.tensor_tensor(o[:, t % 2].rearrange("p (h d) -> p h d", d=HD), heads[:, :, 0:HD],
                                        z[:, :].unsqueeze(2).broadcast_to([P, HEADS, HD]), ALU.mult).then_inc(o_ready, 1)

            def add_bias(b, t):
                n = b * BT + t
                dve.wait_ge(out_done, n + 1)
                dve.wait_ge(delta_free, n + 1)
                s = (QKV_UNITS + t) % 2
                nc.vector.tensor_tensor(delta[:, t % 2], psQ[:, s, 0:DIM], bout[:, :], ALU.add).then_inc(delta_ready, 1)
                dve.wait_ge(delta_ready, n + 1)
                dve.sem_inc(slot_free[s], 1)

            dve.sem_inc(psF_free, 2)
            nc.vector.memset(proj_diag[:, :, :], 0.0).then_inc(diag_zero, 1)
            nc.vector.memset(v_one[:, :, :, HD:V1], 1.0).then_inc(ones_set, 1)
            nc.vector.memset(kv[:, :, :], 0.0).then_inc(ones_set, 1)
            dve.wait_ge(const_in, 16 * 3)
            with dve.Fori(0, BATCH) as b:
                for k in range(BT):
                    t = b * BT + k
                    last = nc.vector.tensor_scalar(
                        xn[:, k, :], g.x[:, bass.ds(t, 1), :].rearrange("p a d -> p (a d)"),
                        g.aggr[:, bass.ds(t, 1), 0], g.rstd[:, bass.ds(t, 1)], ALU.subtract, ALU.mult)
                    if k % CT == CT - 1:
                        last.then_inc(xn_ready, 1)
                for u in range(K_UNITS):
                    feature(b, u)
                less_than_zero(b, K_UNITS)
                for u in range(K_UNITS, UNITS):
                    if u + 1 < UNITS:
                        less_than_zero(b, u + 1)
                    feature(b, u)
                for t in range(BT):
                    normalise(b, t)
                    if t >= 2:
                        add_bias(b, t - 2)
                add_bias(b, BT - 2)
                add_bias(b, BT - 1)

        @block.gpsimd
        def _(pool):
            pool.sem_inc(delta_free, 2)
            with pool.Fori(0, BATCH) as b:
                for t in range(BT):
                    n = b * BT + t
                    pool.wait_ge(delta_ready, n + 1)
                    xs = g.x[:, bass.ds(n, 1), :].rearrange("p a d -> p (a d)")
                    nc.gpsimd.tensor_tensor(xs, xs, delta[:, t % 2], ALU.add).then_inc(delta_free, 1)

        @block.scalar
        def _(act):
            act.sem_inc(psT_free, 1)
            act.sem_inc(slot_free[0], 1)
            act.sem_inc(slot_free[1], 1)
            act.wait_ge(ones_set, 2)
            with act.Fori(0, BATCH) as b:
                for h in range(HB):
                    act.wait_ge(transposed, b * HB + (h + 1))
                    nc.scalar.copy(xT[:, :, :], psT[:, :, :]).then_inc(xT_ready, 1)
                    act.wait_ge(xT_ready, b * HB + (h + 1))
                    act.sem_inc(psT_free, 1)
                    for k in range(6):
                        u = h * 6 + k
                        act.wait_ge(proj_done, b * QKV_UNITS + (u + 1))
                        if k < 2 * KC:
                            into = (qT if k < KC else kT)[:, k % KC, h * CHUNK:(h + 1) * CHUNK]
                            source = psQ[:, u % 2, :]
                        else:
                            t = h * CT + (k - 2 * KC) * 2
                            into = v_one[:, t:t + 2, :, 0:HD]
                            source = psQ[:, u % 2, :].rearrange("p (t h d) -> p t h d", t=2, d=HD)
                        nc.scalar.copy(into, source).then_inc(qkv_ready, 1)
                        act.wait_ge(qkv_ready, b * QKV_UNITS + (u + 1))
                        act.sem_inc(slot_free[u % 2], 1)
                for u in range(UNITS):
                    if u < K_UNITS:
                        act.wait_ge(feat_done, b * UNITS + (u + 1))
                        nc.scalar.activation(negative[:, u % 2, :], psF[:, u % 2, :], ACT.Relu, scale=-1.0).then_inc(negative_ready, 1)
                    act.wait_ge(negative_ready, b * UNITS + (u + 1))
                    nc.scalar.activation(exped[:, u % 2, :], negative[:, u % 2, :], ACT.Exp, scale=-1.0 if u < K_UNITS else 1.0).then_inc(exp_ready, 1)
                act.wait_ge(kv_done, b + 1)
                for m in range(2):
                    rows, cols = slice(m * FEAT, (m + 1) * FEAT), slice(m * V1, (m + 1) * V1)
                    nc.scalar.copy(kv[rows, :, cols], psKV[rows, :, cols]).then_inc(kv_ready, 1)
                for t in range(BT):
                    act.wait_ge(o_transposed, b * BT + (t + 1))
                    nc.scalar.copy(oT[:, t % 2], psT[:, :, 0:P]).then_inc(oT_ready, 1)
                    act.wait_ge(oT_ready, b * BT + (t + 1))
                    act.sem_inc(psT_free, 1)

        @block.tensor
        def _(pe):
            def output(b, t):
                u = QKV_UNITS + t
                pe.wait_ge(oT_ready, b * BT + (t + 1))
                pe.wait_ge(slot_free[u % 2], b * SLOT_USES + (u // 2 + 1))
                for c in range(KC):
                    last = nc.tensor.matmul(psQ[:, u % 2, 0:DIM], oT[:, t % 2, c, :], wout[:, c, :], start=c == 0, stop=c == KC - 1)
                last.then_inc(out_done, 1)

            def transpose_o(b, t):
                pe.wait_ge(o_ready, b * BT + (t + 1))
                pe.wait_ge(psT_free, b * T_USES + (HB + t + 1))
                for c in range(KC):
                    last = nc.tensor.transpose(psT[:, c, 0:P], o[:, t % 2, c * P:(c + 1) * P], g.ident[:, :])
                last.then_inc(o_transposed, 1)

            pe.wait_ge(const_in, 16 * 3)
            pe.wait_ge(diag_in, 16 * HEADS)
            with pe.Fori(0, BATCH) as b:
                for h in range(HB):
                    n = b * HB + h
                    pe.wait_ge(xn_ready, n + 1)
                    pe.wait_ge(psT_free, b * T_USES + (h + 1))
                    for t in range(CT):
                        for c in range(KC):
                            last = nc.tensor.transpose(psT[:, c, t * P:(t + 1) * P], xn[:, h * CT + t, c * P:(c + 1) * P], g.ident[:, :])
                    last.then_inc(transposed, 1)
                    pe.wait_ge(xT_ready, n + 1)
                    for k in range(6):
                        u = h * 6 + k
                        pe.wait_ge(slot_free[u % 2], b * SLOT_USES + (u // 2 + 1))
                        if k < 2 * KC:
                            for c in range(KC):
                                last = nc.tensor.matmul(psQ[:, u % 2, :], wqkv[:, c, k * P:(k + 1) * P], xT[:, c, :], start=c == 0, stop=c == KC - 1)
                        else:
                            for m in range(2):
                                t = (k - 2 * KC) * 2 + m
                                for c in range(KC):
                                    last = nc.tensor.matmul(psQ[:, u % 2, m * DIM:(m + 1) * DIM], xT[:, c, t * P:(t + 1) * P], wqkv[:, c, 2 * DIM:3 * DIM], start=c == 0, stop=c == KC - 1)
                        last.then_inc(proj_done, 1)
                pe.wait_ge(qkv_ready, b * QKV_UNITS + QKV_UNITS)
                for u in range(UNITS):
                    pe.wait_ge(psF_free, b * UNITS + (u + 1))
                    if u < K_UNITS:
                        t, c = divmod(u, KC)
                        nc.tensor.matmul(psF[:, u % 2, :], kT[:, c, t * P:(t + 1) * P], proj_diag[:, c, :], start=True, stop=True).then_inc(feat_done, 1)
                    else:
                        h, pair = divmod(u - K_UNITS, PAIRS)
                        c, m = divmod(pair, PAIRS // KC)
                        nc.tensor.matmul(psF[:, u % 2, :], proj_diag[:, c, m * P:(m + 1) * P], qT[:, c, h * CHUNK:(h + 1) * CHUNK], start=True, stop=True).then_inc(feat_done, 1)
                pe.wait_ge(psF_free, b * UNITS + (K_UNITS + 2))
                for pair in range(PAIRS):
                    for t in range(BT):
                        last = nc.tensor.matmul(psKV[:, pair, :], k_feat[:, t, pair * P:(pair + 1) * P],
                                                v_one[:, t, 2 * pair:2 * pair + 2, :].rearrange("p h v -> p (h v)"), start=t == 0, stop=t == BT - 1)
                last.then_inc(kv_done, 1)
                pe.wait_ge(psF_free, b * UNITS + (UNITS + 2))
                pe.wait_ge(kv_ready, b * 2 + 2)
                for t in range(BT):
                    if t:
                        pe.wait_ge(o_ready, b * BT + t)
                    for pair in range(PAIRS):
                        last = nc.tensor.matmul(psO[:, pair, :], q_feat[:, pair, t * P:(t + 1) * P], kv[:, pair, :], start=True, stop=True)
                    last.then_inc(attended, 1)
                    if t >= 1:
                        transpose_o(b, t - 1)
                    if t >= 2:
                        output(b, t - 2)
                transpose_o(b, BT - 1)
                output(b, BT - 2)
                output(b, BT - 1)


EXPERTS = 8
PER_GROUP = 2
FFN = int(DIM * 4 * (2.0 / 3.0))
FB = (FFN + P - 1) // P
FLAST = FFN - (FB - 1) * P
CAPACITY = TILES * P // EXPERTS
EC = CAPACITY // P
ROW = DIM + EXPERTS
BLOCKED = 4096.0


def route(nc, g, name, w_r, b_r, rows_dram, iota128, tri, seg, tok_p, tok_t):
    layernorm_stats(nc, g, f"{name}_ln")
    with ExitStack() as ctx:
        sb = lambda n, s, d=F32: ctx.enter_context(nc.sbuf_tensor(f"{name}_{n}", s, d))
        ps = lambda n, s: ctx.enter_context(nc.psum_tensor(f"{name}_{n}", s, F32))
        sem = ctx.enter_context(stage_semaphores(nc, name))
        ET = EXPERTS * TILES
        wr = sb("wr", [P, KC, EXPERTS])
        br = sb("br", [P, EXPERTS])
        iota_row = sb("iota_row", [P, P])
        tri_sb = sb("tri", [P, P])
        tri_bf = sb("tri_bf", [P, P], BF16)
        ones_bf = sb("ones_bf", [P, P], BF16)
        segment = sb("segment", [P, 2 * ET])
        tokp = sb("tokp", [P, 1])
        tokt = sb("tokt", [P, EXPERTS, TILES])
        xT = sb("xT", [P, 2, 4, KC, P])
        logit = sb("logit", [P, TILES, EXPERTS])
        top = sb("top", [P, TILES])
        prob = sb("prob", [P, EXPERTS, TILES])
        ge = sb("ge", [P, EXPERTS, TILES])
        count = sb("count", [P, EXPERTS], BF16)
        thr = sb("thr", [P, EXPERTS])
        base = sb("base", [P, EXPERTS])
        cand = sb("cand", [P, EXPERTS])
        kept = sb("kept", [P, EXPERTS])
        mask = sb("mask", [P, 2, EXPERTS, TILES], BF16)
        total = sb("total", [P, 2, EXPERTS, TILES])
        running = sb("running", [P, 2, EXPERTS, TILES])
        before = sb("before", [P, 2, EXPERTS, TILES])
        pos = sb("pos", [P, EXPERTS, TILES])
        hi = sb("hi", [P, EXPERTS, TILES])
        low = sb("low", [P, EXPERTS, TILES])
        values = sb("values", [P, EXPERTS, TILES, EC, 2], BF16)
        onehot = sb("onehot", [P, 2, TILES, P], BF16)
        psT = ps("psT", [P, 2, 4, KC, P])
        psR = ps("psR", [P, TILES, EXPERTS])
        psC = ps("psC", [P, 512])
        psI = ps("psI", [P, EXPERTS, EC, 2])

        const_in = sem("const_in")
        const_ready = sem("const_ready")
        xn_ready = sem("xn_ready")
        transposed = sem("transposed")
        xT_ready = sem("xT_ready")
        routed = sem("routed")
        shifted = sem("shifted")
        exp_ready = sem("exp_ready")
        step_done = sem("dve_step")
        counted = sem("counted")
        summed = sem("summed")
        masks_ready = sem("masks_ready")
        prefix_done = sem("prefix_done")
        total_ready = sem("total_ready")
        values_ready = sem("values_ready")
        onehot_ready = sem("onehot_ready")
        listed = sem("listed")
        rows_ready = sem("rows_ready")
        rows_out = sem("rows_out")
        block = ctx.enter_context(nc.Block())
        EXP_STEPS = [64, 32, 16, 8, 4, 2, 1]
        MANTISSA = 23

        @block.sync
        def _(sp):
            for dst, src in ((wr[:, :, :], w_r.rearrange("(c p) e -> p c e", p=P)), (br[:, :], b_r.partition_broadcast(P)),
                             (iota_row[:, :], iota128.partition_broadcast(P)), (tri_sb[:, :], tri),
                             (segment[:, :], seg.partition_broadcast(P)), (tokp[:, :], tok_p),
                             (tokt[:, :, :].rearrange("p e t -> p (e t)"), tok_t.partition_broadcast(P))):
                sp.dma_start(dst, src).then_inc(const_in, 16)
            sp.wait_ge(rows_ready, 1)
            sp.dma_start(rows_dram.rearrange("(t p) r -> p t r", p=P), g.rows[:, :, :]).then_inc(rows_out, 16)
            sp.wait_ge(rows_out, 16)

        @block.vector
        def _(dve):
            dve.wait_ge(const_in, 16 * 7)
            nc.vector.tensor_copy(tri_bf[:, :], tri_sb[:, :]).then_inc(const_ready, 1)
            nc.vector.memset(ones_bf[:, :], 1.0).then_inc(const_ready, 1)
            with dve.Fori(0, TILES // 4) as i:
                for k in range(4):
                    t = i * 4 + k
                    last = nc.vector.tensor_scalar(
                        g.rows[:, bass.ds(t, 1), 0:DIM].rearrange("p a d -> p (a d)"),
                        g.x[:, bass.ds(t, 1), :].rearrange("p a d -> p (a d)"),
                        g.aggr[:, bass.ds(t, 1), 0], g.rstd[:, bass.ds(t, 1)], ALU.subtract, ALU.mult)
                last.then_inc(xn_ready, 1)
            link = chain(dve, step_done)
            dve.wait_ge(routed, TILES // 4)
            link(nc.vector.tensor_tensor(logit[:, :, :], psR[:, :, :], br[:, :].unsqueeze(1).broadcast_to([P, TILES, EXPERTS]), ALU.add))
            link(nc.vector.tensor_reduce(top[:, :], logit[:, :, :], AX_X, ALU.max))
            nc.vector.tensor_tensor(logit[:, :, :], logit[:, :, :], top[:, :].unsqueeze(2).broadcast_to([P, TILES, EXPERTS]), ALU.subtract).then_inc(shifted, 1)
            dve.wait_ge(exp_ready, 1)
            link(nc.vector.tensor_reduce(top[:, :], logit[:, :, :], AX_X, ALU.add))
            link(nc.vector.reciprocal(top[:, :], top[:, :]))
            link(nc.vector.tensor_tensor(prob[:, :, :].rearrange("p e t -> p t e"), logit[:, :, :], top[:, :].unsqueeze(2).broadcast_to([P, TILES, EXPERTS]), ALU.mult))
            nc.vector.tensor_copy(g.rows[:, :, DIM:ROW], prob[:, :, :].rearrange("p e t -> p t e")).then_inc(rows_ready, 1)
            link(nc.vector.memset(thr[:, :], 2.0 ** -126))
            link(nc.vector.tensor_scalar(cand[:, :], thr[:, :], 2.0 ** EXP_STEPS[0], None, ALU.mult))

            def at_or_above():
                link(nc.vector.tensor_tensor(ge[:, :, :], prob[:, :, :], cand[:, :].unsqueeze(2).broadcast_to([P, EXPERTS, TILES]), ALU.is_ge))
                nc.vector.tensor_reduce(count[:, :], ge[:, :, :], AX_X, ALU.add).then_inc(counted, 1)

            def keep():
                link(nc.vector.scalar_tensor_tensor(kept[:, :], psC[:, 0:EXPERTS], float(CAPACITY), cand[:, :], ALU.is_ge, ALU.mult))
                link(nc.vector.tensor_tensor(thr[:, :], thr[:, :], kept[:, :], ALU.max))

            with nc.allow_low_precision(reason="counts of at most 32 are exact in bfloat16"):
                for k, e in enumerate(EXP_STEPS):
                    at_or_above()
                    dve.wait_ge(summed, k + 1)
                    keep()
                    if k + 1 < len(EXP_STEPS):
                        link(nc.vector.tensor_scalar(cand[:, :], thr[:, :], 2.0 ** EXP_STEPS[k + 1], None, ALU.mult))
                link(nc.vector.tensor_scalar(base[:, :], thr[:, :], 0.5, None, ALU.mult))
                for k in range(MANTISSA):
                    link(nc.vector.scalar_tensor_tensor(cand[:, :], base[:, :], 2.0 ** -k, thr[:, :], ALU.mult, ALU.add))
                    at_or_above()
                    dve.wait_ge(summed, len(EXP_STEPS) + k + 1)
                    keep()
                link(nc.vector.tensor_copy(cand[:, :], thr[:, :]))
                at_or_above()
                dve.wait_ge(summed, len(EXP_STEPS) + MANTISSA + 1)
                link(nc.vector.scalar_tensor_tensor(thr[:, :], psC[:, 0:EXPERTS], float(CAPACITY), cand[:, :], ALU.is_ge, ALU.mult))
            wide = thr[:, :].unsqueeze(2).broadcast_to([P, EXPERTS, TILES])
            nc.vector.tensor_tensor(mask[:, 0], prob[:, :, :], wide, ALU.is_gt).then_inc(masks_ready, 1)
            nc.vector.tensor_tensor(mask[:, 1], prob[:, :, :], wide, ALU.is_equal).then_inc(masks_ready, 1)
            dve.wait_ge(masks_ready, 2)
            flat = lambda a: a.rearrange("p m e t -> p (m e t)")
            dve.wait_ge(prefix_done, 1)
            link(nc.vector.tensor_copy(flat(total[:, :, :, :]), psC[:, :]))
            dve.sem_inc(total_ready, 1)
            link(nc.vector.tensor_tensor_scan(flat(running[:, :, :, :]), segment[:, :], flat(total[:, :, :, :]), 0.0, ALU.mult, ALU.add))
            link(nc.vector.tensor_tensor(flat(before[:, :, :, :]), flat(running[:, :, :, :]), flat(total[:, :, :, :]), ALU.subtract))
            dve.wait_ge(prefix_done, 2)
            link(nc.vector.tensor_tensor(flat(before[:, :, :, :]), flat(before[:, :, :, :]), psC[:, :], ALU.add))
            link(nc.vector.tensor_tensor(before[:, 1], before[:, 1], running[:, 0, :, TILES - 1:TILES].broadcast_to([P, EXPERTS, TILES]), ALU.add))
            link(nc.vector.tensor_tensor(before[:, :, :, :], before[:, :, :, :], mask[:, :, :, :], ALU.mult))
            link(nc.vector.tensor_tensor(pos[:, :, :], before[:, 0], before[:, 1], ALU.add))
            link(nc.vector.tensor_tensor(hi[:, :, :], mask[:, 0], mask[:, 1], ALU.add))
            link(nc.vector.tensor_scalar(hi[:, :, :], hi[:, :, :], -BLOCKED, BLOCKED, ALU.mult, ALU.add))
            link(nc.vector.tensor_tensor(pos[:, :, :], pos[:, :, :], hi[:, :, :], ALU.add))
            link(nc.vector.tensor_scalar(hi[:, :, :], pos[:, :, :], float(P), None, ALU.is_ge))
            for k in range(2, EC):
                link(nc.vector.scalar_tensor_tensor(hi[:, :, :], pos[:, :, :], float(k * P), hi[:, :, :], ALU.is_ge, ALU.add))
            link(nc.vector.scalar_tensor_tensor(low[:, :, :], hi[:, :, :], -float(P), pos[:, :, :], ALU.mult, ALU.add))
            for k in range(EC):
                nc.vector.tensor_scalar(values[:, :, :, k, 0], hi[:, :, :], float(k), tokp[:, 0:1], ALU.is_equal, ALU.mult).then_inc(values_ready, 1)
                nc.vector.scalar_tensor_tensor(values[:, :, :, k, 1], hi[:, :, :], float(k), tokt[:, :, :], ALU.is_equal, ALU.mult).then_inc(values_ready, 1)
            for e in range(EXPERTS):
                if e >= 2:
                    dve.wait_ge(listed, e - 1)
                nc.vector.tensor_tensor(onehot[:, e % 2], low[:, e, :].unsqueeze(2).broadcast_to([P, TILES, P]),
                                        iota_row[:, :].unsqueeze(1).broadcast_to([P, TILES, P]), ALU.is_equal).then_inc(onehot_ready, 1)
            dve.wait_ge(listed, EXPERTS)
            link(nc.vector.tensor_copy(before[:, 0, :, 0:EC * 2].rearrange("p e (k v) -> p e k v", v=2), psI[:, :, :, :]))
            got = before[:, 0, :, 0:EC * 2].rearrange("p e (k v) -> p e k v", v=2)
            link(nc.vector.scalar_tensor_tensor(g.index[:, :].rearrange("p (e k) -> p e k", k=EC), got[:, :, :, 1], float(P), got[:, :, :, 0], ALU.mult, ALU.add))

        @block.scalar
        def _(act):
            with act.Fori(0, TILES // 8) as i:
                for slot in range(2):
                    act.wait_ge(transposed, i * 2 + slot + 1)
                    nc.scalar.copy(xT[:, slot], psT[:, slot]).then_inc(xT_ready, 1)
            act.wait_ge(shifted, 1)
            nc.scalar.activation(logit[:, :, :], logit[:, :, :], ACT.Exp).then_inc(exp_ready, 1)

        @block.tensor
        def _(pe):
            def transposes(n, slot):
                pe.wait_ge(xn_ready, n + 1)
                for k in range(4):
                    for c in range(KC):
                        last = nc.tensor.transpose(psT[:, slot, k, c, :], g.rows[:, n * 4 + k, c * P:(c + 1) * P], g.ident[:, :])
                last.then_inc(transposed, 1)

            pe.wait_ge(const_ready, 2)
            for n in range(TILES // 4):
                slot = n % 2
                if n >= 2:
                    pe.wait_ge(xT_ready, n - 1)
                transposes(n, slot)
                pe.wait_ge(xT_ready, n + 1)
                for k in range(4):
                    for c in range(KC):
                        last = nc.tensor.matmul(psR[:, n * 4 + k, :], xT[:, slot, k, c, :], wr[:, c, :], start=c == 0, stop=c == KC - 1)
                last.then_inc(routed, 1)
            for k in range(len(EXP_STEPS) + MANTISSA + 1):
                pe.wait_ge(counted, k + 1)
                nc.tensor.matmul(psC[:, 0:EXPERTS], ones_bf[:, :], count[:, :], start=True, stop=True).then_inc(summed, 1)
            pe.wait_ge(masks_ready, 2)
            flat = mask[:, :, :, :].rearrange("p m e t -> p (m e t)")
            nc.tensor.matmul(psC[:, :], ones_bf[:, :], flat, start=True, stop=True).then_inc(prefix_done, 1)
            pe.wait_ge(total_ready, 1)
            nc.tensor.matmul(psC[:, :], tri_bf[:, :], flat, start=True, stop=True).then_inc(prefix_done, 1)
            pe.wait_ge(values_ready, 2 * EC)
            for e in range(EXPERTS):
                pe.wait_ge(onehot_ready, e + 1)
                for t in range(TILES):
                    last = nc.tensor.matmul(psI[:, e].rearrange("p k v -> p (k v)"), onehot[:, e % 2, t, :],
                                            values[:, e, t].rearrange("p k v -> p (k v)"), start=t == 0, stop=t == TILES - 1)
                last.then_inc(listed, 1)


def experts(nc, g, name, x_dram, rows_dram, w_up, b_up, w_down, b_down):
    with ExitStack() as ctx:
        sb = lambda n, s, d=F32: ctx.enter_context(nc.sbuf_tensor(f"{name}_{n}", s, d))
        ps = lambda n, s: ctx.enter_context(nc.psum_tensor(f"{name}_{n}", s, F32))
        sem = ctx.enter_context(stage_semaphores(nc, name))
        rows = sb("rows", [P, EXPERTS * EC, ROW])
        rowsT = sb("rowsT", [P, KC, CAPACITY])
        wup = sb("wup", [P, KC, FFN])
        bup = sb("bup", [P, FB, EXPERTS // PER_GROUP])
        wdown = sb("wdown", [P, PER_GROUP, FB, DIM])
        bdown = sb("bdown", [P, EXPERTS, DIM])
        hidden = sb("hidden", [P, 2, FB, CAPACITY])
        y = sb("y", [P, 2, EC, DIM])
        psT = ps("psT", [P, KC, CAPACITY])
        psU = ps("psU", [P, 2, CAPACITY])
        psD = ps("psD", [P, EC, DIM])

        const_in = sem("const_in")
        gathered = [sem(f"gathered{e}") for e in range(EXPERTS)]
        gathered_all = sem("gathered_all")
        up_in = sem("up_in")
        down_in = [sem(f"down_in{m}") for m in range(PER_GROUP)]
        transposed = sem("transposed")
        rowsT_ready = sem("rowsT_ready")
        up_done = sem("up_done")
        hidden_ready = sem("hidden_ready")
        down_done = sem("down_done")
        y_bias = sem("y_bias")
        y_ready = sem("y_ready")
        added = sem("added")
        credits = sem("credits")
        block = ctx.enter_context(nc.Block())
        GROUPS_ = EXPERTS // PER_GROUP
        size = lambda f: P if f < FB - 1 else FLAST

        @block.sync
        def _(sp):
            full = (FB - 1) * P
            sp.dma_start(bup[:, 0:FB - 1, :], b_up[0:full, :].rearrange("(f p) g -> p f g", p=P)).then_inc(const_in, 16)
            sp.dma_start(bup[0:FLAST, FB - 1, :], b_up[full:FFN, :]).then_inc(const_in, 16)
            sp.dma_start(bdown[:, :, :].rearrange("p e d -> p (e d)"), b_down.partition_broadcast(P)).then_inc(const_in, 16)
            for gr in range(GROUPS_):
                if gr:
                    sp.wait_ge(up_done, gr * PER_GROUP * FB)
                sp.dma_start(wup[:, :, :], w_up[gr].rearrange("(c p) f -> p c f", p=P)).then_inc(up_in, 16)
                for m in range(PER_GROUP):
                    e = gr * PER_GROUP + m
                    if gr:
                        sp.wait_ge(down_done, e - PER_GROUP + 1)
                    sp.dma_start(wdown[:, m, 0:FB - 1, :], w_down[e, 0:full, :].rearrange("(f p) d -> p f d", p=P)).then_inc(down_in[m], 16)
                    sp.dma_start(wdown[0:FLAST, m, FB - 1, :], w_down[e, full:FFN, :]).then_inc(down_in[m], 16)

        @block.gpsimd
        def _(pool):
            for e in range(EXPERTS):
                for k in range(EC):
                    c = e * EC + k
                    nc.gpsimd.indirect_dma_start(
                        rows[:, c, :], None, rows_dram, bass.IndirectOffsetOnAxis(ap=g.index[:, c:c + 1], axis=0)).then_inc(gathered[e], 16)
            for e in range(EXPERTS):
                pool.wait_ge(y_ready, e + 1)
                if e:
                    pool.wait_ge(added, e * EC * 16)
                for k in range(EC):
                    c = e * EC + k
                    nc.gpsimd.indirect_dma_start(
                        x_dram, bass.IndirectOffsetOnAxis(ap=g.index[:, c:c + 1], axis=0), y[:, e % 2, k, :], None,
                        compute_op=ALU.add).then_inc(added, 16)
            pool.wait_ge(added, EXPERTS * EC * 16)

        @block.vector
        def _(dve):
            dve.wait_ge(const_in, 48)
            for e in range(EXPERTS):
                slot = e % 2
                dve.wait_ge(down_done, e + 1)
                if e >= 2:
                    dve.wait_ge(added, (e - 1) * EC * 16)
                nc.vector.tensor_tensor(y[:, slot], psD[:, :, :], bdown[:, e, :].unsqueeze(1).broadcast_to([P, EC, DIM]), ALU.add).then_inc(y_bias, 1)
                dve.wait_ge(y_bias, e + 1)
                for k in range(EC):
                    c = e * EC + k
                    last = nc.vector.tensor_scalar(y[:, slot, k, :], y[:, slot, k, :], rows[:, c, DIM + e:DIM + e + 1], 0.5, ALU.mult, ALU.mult)
                last.then_inc(y_ready, 1)

        @block.scalar
        def _(act):
            act.wait_ge(const_in, 48)
            for e in range(EXPERTS):
                act.wait_ge(transposed, e + 1)
                nc.scalar.copy(rowsT[:, :, :], psT[:, :, :]).then_inc(rowsT_ready, 1)
                for f in range(FB):
                    n = e * FB + f
                    act.wait_ge(up_done, n + 1)
                    if e >= 2 and f == 0:
                        act.wait_ge(down_done, e - 1)
                    nc.scalar.activation(hidden[0:size(f), e % 2, f, :], psU[0:size(f), n % 2, :], ACT.Silu,
                                         bias=bup[0:size(f), f, e // PER_GROUP:e // PER_GROUP + 1]).then_inc(hidden_ready, 1)

        @block.tensor
        def _(pe):
            def take(e):
                pe.wait_ge(gathered[e], EC * 16)
                if e:
                    pe.wait_ge(rowsT_ready, e)
                for k in range(EC):
                    for c in range(KC):
                        last = nc.tensor.transpose(psT[:, c, k * P:(k + 1) * P], rows[:, e * EC + k, c * P:(c + 1) * P], g.ident[:, :])
                last.then_inc(transposed, 1)

            def up(e):
                pe.wait_ge(up_in, (e // PER_GROUP + 1) * 16)
                pe.wait_ge(rowsT_ready, e + 1)
                for f in range(FB):
                    n = e * FB + f
                    if n >= 2:
                        pe.wait_ge(hidden_ready, n - 1)
                    for c in range(KC):
                        last = nc.tensor.matmul(psU[0:size(f), n % 2, :], wup[:, c, f * P:f * P + size(f)], rowsT[:, c, :], start=c == 0, stop=c == KC - 1)
                    last.then_inc(up_done, 1)

            def down(e):
                pe.wait_ge(down_in[e % PER_GROUP], (e // PER_GROUP + 1) * 32)
                pe.wait_ge(hidden_ready, (e + 1) * FB)
                if e:
                    pe.wait_ge(y_ready, e)
                for k in range(EC):
                    for f in range(FB):
                        last = nc.tensor.matmul(psD[:, k, :], hidden[0:size(f), e % 2, f, k * P:(k + 1) * P], wdown[0:size(f), e % PER_GROUP, f, :],
                                                start=f == 0, stop=f == FB - 1)
                last.then_inc(down_done, 1)

            take(0)
            up(0)
            for e in range(EXPERTS):
                if e + 1 < EXPERTS:
                    take(e + 1)
                    up(e + 1)
                down(e)


def moe(nc, g, name, a, x_dram, x_from, rows_dram):
    with ExitStack() as ctx:
        g.index = ctx.enter_context(nc.sbuf_tensor(f"{name}_index", [P, EXPERTS * EC], I32))
        with residual(nc, g, name):
            with ExitStack() as c2:
                g.rows = c2.enter_context(nc.sbuf_tensor(f"{name}_rows", [P, TILES, ROW], F32))
                setup(nc, g, name, x_from)
                route(nc, g, f"{name}_r", a["Wr"], a["br"], rows_dram, a["iota"], a["tri"], a["seg"], a["tok_p"], a["tok_t"])
        experts(nc, g, f"{name}_x", x_dram, rows_dram, a["W_up"], a["b_up"], a["W_down"], a["b_down"])



ALL_STAGES = ("moe1", "attn", "moe2", "mix1", "lin", "mix2")


def program(nc, a, out, stages=ALL_STAGES):
    with ExitStack() as ctx:
        g = Common()
        g.ident = ctx.enter_context(nc.sbuf_tensor("ident", [P, P], F32))
        x_dram = nc.dram_tensor("x_scratch", [TILES * P, DIM], F32).ap()
        rows_dram = nc.dram_tensor("rows_scratch", [TILES * P, ROW], F32).ap()
        copy_in(nc, g, "in", x_dram, a["x"], a["ident"])
        if "moe1" in stages:
            moe(nc, g, "moe1", a, x_dram, x_dram, rows_dram)
        if "attn" in stages:
            talking_heads(nc, g, x_dram, a["Wqkv"], a["bqkv"], a["Wpre"], a["Wpost"], a["Wpost_all"], a["Wout"], a["bout"], a["cos"], a["sin"], a["same_token"])
        if "moe2" in stages:
            moe(nc, g, "moe2", a, x_dram, x_dram, rows_dram)
        with residual(nc, g, "last"):
            setup(nc, g, "last", x_dram)
            if "mix1" in stages:
                channel_mix(nc, g, "mix1", a["W_r"], a["W_k"], a["W_v"], a["mu_r"], a["mu_k"])
            if "lin" in stages:
                linear_attention(nc, g, "lin", a["w_qkv"], a["proj_matrix"], a["w_out"], a["b_out"])
            if "mix2" in stages:
                channel_mix(nc, g, "mix2", a["W_r"], a["W_k"], a["W_v"], a["mu_r"], a["mu_k"])
            store(nc, g, out)


def kernel(**inputs):
    import numpy as _np
    import concourse.bacc as _bacc
    from concourse import mybir as _mybir
    from concourse.bass_utils import run_bass_kernel_spmd as _run

    f32 = _np.float32
    w = {name: _np.asarray(value) for name, value in inputs.items()}
    inv = (1.0 / f32(10000.0) ** (_np.arange(0, HD, 2, dtype=f32) / f32(HD))).astype(f32)
    angle = (_np.arange(SEQ, dtype=f32)[:, None] * inv[None, :]).astype(f32).astype(_np.float64)
    arrays = {
        "x": w["L0_attn_x"].reshape(BATCH * SEQ, DIM),
        "Wqkv": w["L0_attn_Wqkv"].T,
        "bqkv": w["L0_attn_bqkv"],
        "Wpre": _np.repeat(w["L0_attn_Wpre"].T, HD, axis=0),
        "Wpost": _np.repeat(w["L0_attn_Wpost"].T, GI, axis=0),
        "Wpost_all": w["L0_attn_Wpost"].reshape(-1),
        "Wout": _np.repeat(w["L0_attn_Wout"].T.reshape(OC, HEADS // OC, 1, HD, DIM), 2, axis=2).reshape(OC, P, DIM).transpose(1, 0, 2),
        "bout": w["L0_attn_bout"],
        "cos": _np.cos(angle).astype(f32),
        "sin": _np.sin(angle).astype(f32),
        "same_token": _np.tile(_np.eye(GI, dtype=f32), (HEADS, HEADS)),
        "ident": _np.eye(P, dtype=f32),
        "Wr": w["L0_ffn_Wr"],
        "br": w["L0_ffn_br"],
        "W_up": w["L0_ffn_W_up"],
        "b_up": w["L0_ffn_b_up"].T,
        "W_down": w["L0_ffn_W_down"],
        "b_down": w["L0_ffn_b_down"].reshape(-1),
        "iota": _np.arange(P, dtype=f32),
        "tri": _np.triu(_np.ones((P, P), f32), 1),
        "seg": _np.tile((_np.arange(TILES) > 0).astype(f32), 2 * EXPERTS),
        "tok_p": _np.arange(P, dtype=f32)[:, None],
        "tok_t": _np.tile(_np.arange(TILES, dtype=f32), EXPERTS),
        "w_qkv": w["L1_attn_w_qkv"],
        "proj_matrix": w["L1_attn_proj_matrix"],
        "w_out": w["L1_attn_w_out"],
        "b_out": w["L1_attn_b_out"],
        "W_r": w["L1_ffn_W_r"].T,
        "W_k": w["L1_ffn_W_k"].T,
        "W_v": w["L1_ffn_W_v"].T,
        "mu_r": w["L1_ffn_mu_r"].reshape(KC, P).T,
        "mu_k": w["L1_ffn_mu_k"].reshape(KC, P).T,
    }
    nc = _bacc.Bacc("TRN2", target_bir_lowering=False, num_devices=1)
    feed, args = {}, {}
    for name, array in arrays.items():
        array = _np.ascontiguousarray(array)
        feed[f"in_{name}"] = array
        args[name] = nc.dram_tensor(f"in_{name}", array.shape, _mybir.dt.from_np(array.dtype), kind="ExternalInput").ap()
    out = nc.dram_tensor("out", (BATCH * SEQ, DIM), F32, kind="ExternalOutput").ap()
    program(nc, args, out)
    r = _run(nc, [feed], core_ids=[0])
    return r.results[0]["out"].reshape(BATCH, SEQ, DIM)
```

```python
import math
from contextlib import ExitStack, contextmanager

import concourse.bass as bass
from concourse import mybir

P = 128
ALU = mybir.AluOpType
ACT = mybir.ActivationFunctionType
F32 = mybir.dt.float32
BF16 = mybir.dt.bfloat16
I32 = mybir.dt.int32
AX_X = mybir.AxisListType.X

BATCH, SEQ, DIM = 4, 1024, 256
KC = DIM // P
TILES = BATCH * SEQ // P
CHUNK = 512
CT = CHUNK // P
CHUNKS = BATCH * SEQ // CHUNK
LN_EPS = 1e-5


class Common:
    pass


def chain(engine, sem):
    count = [0]

    def link(instruction):
        count[0] += 1
        instruction.then_inc(sem, 1)
        engine.wait_ge(sem, count[0])

    return link


@contextmanager
def stage_semaphores(nc, name):
    taken = []

    def sem(n):
        taken.append(nc.alloc_semaphore(name=f"{name}_{n}"))
        return taken[-1]

    yield sem
    nc.clear_and_free_semaphores(taken)
    nc.all_engine_barrier()


class TokenNorm:

    def __init__(self, nc, g, sem, x_in=None):
        self.nc, self.g, self.x_in = nc, g, x_in
        self.x_in_done = [sem(f"x_in{b}") for b in range(BATCH)]
        self.half_set = sem("half_set")
        self.stats_ready = sem("stats_ready")
        self.aggr_ready = sem("aggr_ready")
        self.variance_ready = sem("variance_ready")
        self.rstd_ready = sem("rstd_ready")

    def load(self, sp):
        if self.x_in is not None:
            per = TILES // BATCH
            for b in range(BATCH):
                sp.dma_start(self.g.x[:, b * per:(b + 1) * per, :],
                             self.x_in[b * SEQ:(b + 1) * SEQ, :].rearrange("(t p) d -> p t d", p=P)).then_inc(self.x_in_done[b], 16)

    def statistics(self, dve):
        nc, g = self.nc, self.g
        nc.vector.memset(g.minus_half[:, :], -0.5).then_inc(self.half_set, 1)
        for t in range(TILES):
            if self.x_in is not None and t % (TILES // BATCH) == 0:
                dve.wait_ge(self.x_in_done[t // (TILES // BATCH)], 16)
            nc.vector.bn_stats(g.stats[:, t, :], g.x[:, t, :]).then_inc(self.stats_ready, 1)
        dve.wait_ge(self.stats_ready, TILES)
        for t in range(TILES):
            nc.vector.bn_aggr(g.aggr[:, t, :], g.stats[:, t, :]).then_inc(self.aggr_ready, 1)
        dve.wait_ge(self.aggr_ready, TILES)
        nc.vector.tensor_scalar(g.var_eps[:, :], g.aggr[:, :, 1], LN_EPS, None, ALU.add).then_inc(self.variance_ready, 1)
        dve.wait_ge(self.rstd_ready, 1)

    def roots(self, pool):
        nc, g = self.nc, self.g
        pool.wait_ge(self.half_set, 1)
        pool.wait_ge(self.variance_ready, 1)
        nc.gpsimd.tensor_tensor(g.rstd[:, :], g.var_eps[:, :], g.minus_half[:, :], ALU.pow).then_inc(self.rstd_ready, 1)


@contextmanager
def residual(nc, g, name):
    with ExitStack() as ctx:
        sb = lambda n, s, d=F32: ctx.enter_context(nc.sbuf_tensor(n, s, d))
        g.x = sb(f"{name}_x_residual", [P, TILES, DIM])
        g.stats = sb(f"{name}_ln_stats", [P, TILES, 6])
        g.aggr = sb(f"{name}_ln_aggr", [P, TILES, 2])
        g.var_eps = sb(f"{name}_ln_var_eps", [P, TILES])
        g.rstd = sb(f"{name}_ln_rstd", [P, TILES])
        g.minus_half = sb(f"{name}_minus_half", [P, TILES])
        yield


def store(nc, g, out):
    with ExitStack() as ctx:
        sem = ctx.enter_context(stage_semaphores(nc, "out"))
        stored = sem("x_stored")
        block = ctx.enter_context(nc.Block())

        @block.sync
        def _(sp):
            per = TILES // BATCH
            for b in range(BATCH):
                sp.dma_start(out[b * SEQ:(b + 1) * SEQ, :].rearrange("(t p) d -> p t d", p=P),
                             g.x[:, b * per:(b + 1) * per, :]).then_inc(stored, 16)
            sp.wait_ge(stored, 16 * BATCH)


def channel_mix(nc, g, name, w_r, w_k, w_v, mu_r, mu_k, x_in=None):
    with ExitStack() as ctx:
        sb = lambda n, s, d=F32: ctx.enter_context(nc.sbuf_tensor(f"{name}_{n}", s, d))
        ps = lambda n, s: ctx.enter_context(nc.psum_tensor(f"{name}_{n}", s, F32))
        sem = ctx.enter_context(stage_semaphores(nc, name))
        w = sb("w", [P, 3, KC, DIM])
        mu = sb("mu", [P, 2, KC])
        xn = sb("xn", [P, CT, DIM])
        xT = sb("xT", [P, 2, KC, CHUNK + 1])
        diff = sb("diff", [P, KC, CHUNK])
        xr = sb("xr", [P, 2, KC, CHUNK])
        xk = sb("xk", [P, 2, KC, CHUNK])
        gate = sb("gate", [P, CT, DIM])
        krelu = sb("krelu", [P, KC, CHUNK])
        kact = sb("kact", [P, KC, CHUNK])
        delta = sb("delta", [P, 2, CT, DIM])
        psT = ps("psT", [P, KC, CHUNK])
        psR = ps("psR", [P, CT, DIM])
        psK = ps("psK", [P, KC, CHUNK])
        psV = ps("psV", [P, CT, DIM])

        weights_in = sem("weights_in")
        edge_zero = sem("edge_zero")
        xn_ready = sem("xn_ready")
        transposed = sem("transposed")
        xT_ready = sem("xT_ready")
        diff_ready = sem("diff_ready")
        mixed_ready = sem("mixed_ready")
        r_done = sem("r_done")
        k_done = sem("k_done")
        krelu_ready = sem("krelu_ready")
        kact_ready = sem("kact_ready")
        gate_ready = sem("gate_ready")
        v_done = sem("v_done")
        delta_ready = sem("delta_ready")
        added = sem("added")
        block = ctx.enter_context(nc.Block())
        norm = TokenNorm(nc, g, sem, x_in)
        assert SEQ == 2 * CHUNK

        def chunks(eng, step):
            with eng.Fori(0, CHUNKS // 2 - 1) as i:
                for slot in range(2):
                    step(i * 2 + slot, slot, 2)
            for slot in range(2):
                step(CHUNKS - 2 + slot, slot, 1 - slot)

        @block.sync
        def _(sp):
            norm.load(sp)
            for n, wt in enumerate((w_r, w_k, w_v)):
                sp.dma_start(w[:, n], wt.rearrange("(c p) d -> p c d", p=P)).then_inc(weights_in, 16)
            for n, m in enumerate((mu_r, mu_k)):
                sp.dma_start(mu[:, n, :], m).then_inc(weights_in, 16)

        @block.vector
        def _(dve):
            def normalise(n):
                for t in range(CT):
                    tile = n * CT + t
                    last = nc.vector.tensor_scalar(
                        xn[:, t, :], g.x[:, bass.ds(tile, 1), :].rearrange("p a d -> p (a d)"),
                        g.aggr[:, bass.ds(tile, 1), 0], g.rstd[:, bass.ds(tile, 1)], ALU.subtract, ALU.mult)
                last.then_inc(xn_ready, 1)

            def mix(n, slot):
                dve.wait_ge(diff_ready, n + 1)
                for m, mixed in enumerate((xr, xk)):
                    for c in range(KC):
                        last = nc.vector.scalar_tensor_tensor(
                            mixed[:, slot, c, :], diff[:, c, :], mu[:, m, c:c + 1], xT[:, slot, c, 0:CHUNK], ALU.mult, ALU.add)
                last.then_inc(mixed_ready, 1)

            def step(n, slot, left):
                dve.wait_ge(k_done, n + 1)
                dve.wait_ge(kact_ready, n + 1)
                nc.vector.tensor_scalar(krelu[:, :, :], psK[:, :, :], 0.0, None, ALU.max).then_inc(krelu_ready, 1)
                if left >= 2:
                    dve.wait_ge(transposed, n + 2)
                    normalise(n + 2)
                if left >= 1:
                    mix(n + 1, 1 - slot)
                dve.wait_ge(gate_ready, n + 2)
                dve.wait_ge(v_done, n + 1)
                dve.wait_ge(added, n + 1)
                nc.vector.scalar_tensor_tensor(delta[:, slot], psV[:, :, :], 0.5, gate[:, :, :], ALU.mult, ALU.mult).then_inc(delta_ready, 1)

            dve.sem_inc(delta_ready, 1)
            nc.vector.memset(xT[:, 0, :, 0:1], 0.0).then_inc(edge_zero, 1)
            norm.statistics(dve)
            normalise(0)
            dve.wait_ge(transposed, 1)
            normalise(1)
            dve.wait_ge(weights_in, 16 * 5)
            dve.wait_ge(edge_zero, 1)
            mix(0, 0)
            chunks(dve, step)

        @block.gpsimd
        def _(pool):
            def difference(n, slot):
                pool.wait_ge(xT_ready, n + 2)
                pool.wait_ge(mixed_ready, n + 1)
                nc.gpsimd.tensor_tensor(diff[:, :, :], xT[:, slot, :, 1:CHUNK + 1], xT[:, slot, :, 0:CHUNK], ALU.subtract).then_inc(diff_ready, 1)

            def step(n, slot, left):
                pool.wait_ge(krelu_ready, n + 1)
                pool.wait_ge(delta_ready, n + 1)
                nc.gpsimd.tensor_tensor(kact[:, :, :], krelu[:, :, :], krelu[:, :, :], ALU.mult).then_inc(kact_ready, 1)
                if left >= 1:
                    difference(n + 1, 1 - slot)
                pool.wait_ge(delta_ready, n + 2)
                xs = g.x[:, bass.ds(n * CT, CT), :]
                nc.gpsimd.tensor_tensor(xs, xs, delta[:, slot], ALU.add).then_inc(added, 1)

            pool.sem_inc(added, 2)
            pool.sem_inc(mixed_ready, 1)
            pool.sem_inc(kact_ready, 1)
            norm.roots(pool)
            pool.wait_ge(edge_zero, 1)
            difference(0, 0)
            chunks(pool, step)

        @block.scalar
        def _(act):
            def copy_transposed(n, slot):
                act.wait_ge(transposed, n + 1)
                act.wait_ge(mixed_ready, n + 1)
                if slot == 0:
                    nc.scalar.copy(xT[:, 1, :, 0:1], psT[:, :, CHUNK - 1:CHUNK])
                nc.scalar.copy(xT[:, slot, :, 1:CHUNK + 1], psT[:, :, :]).then_inc(xT_ready, 1)

            def step(n, slot, left):
                if left >= 1:
                    copy_transposed(n + 1, 1 - slot)
                act.wait_ge(r_done, n + 1)
                act.wait_ge(delta_ready, n + 1)
                nc.scalar.activation(gate[:, :, :], psR[:, :, :], ACT.Sigmoid).then_inc(gate_ready, 1)

            act.sem_inc(xT_ready, 1)
            act.sem_inc(gate_ready, 1)
            copy_transposed(0, 0)
            chunks(act, step)

        @block.tensor
        def _(pe):
            def transposes(n):
                pe.wait_ge(xn_ready, n + 1)
                pe.wait_ge(xT_ready, n + 1)
                for t in range(CT):
                    for c in range(KC):
                        last = nc.tensor.transpose(psT[:, c, t * P:(t + 1) * P], xn[:, t, c * P:(c + 1) * P], g.ident[:, :])
                last.then_inc(transposed, 1)

            def step(n, slot, left):
                pe.wait_ge(mixed_ready, n + 2)
                for d in range(KC):
                    for c in range(KC):
                        last = nc.tensor.matmul(psK[:, d, :], w[:, 1, c, d * P:(d + 1) * P], xk[:, slot, c, :], start=c == 0, stop=c == KC - 1)
                last.then_inc(k_done, 1)
                if left >= 1:
                    transposes(n + 1)
                pe.wait_ge(gate_ready, n + 1)
                for t in range(CT):
                    for c in range(KC):
                        last = nc.tensor.matmul(psR[:, t, :], xr[:, slot, c, t * P:(t + 1) * P], w[:, 0, c, :], start=c == 0, stop=c == KC - 1)
                last.then_inc(r_done, 1)
                pe.wait_ge(kact_ready, n + 2)
                pe.wait_ge(delta_ready, n + 1)
                for t in range(CT):
                    for c in range(KC):
                        last = nc.tensor.matmul(psV[:, t, :], kact[:, c, t * P:(t + 1) * P], w[:, 2, c, :], start=c == 0, stop=c == KC - 1)
                last.then_inc(v_done, 1)

            transposes(0)
            pe.wait_ge(weights_in, 16 * 5)
            chunks(pe, step)


HEADS = 16
HD = DIM // HEADS
HALF = HD // 2
SCALE = HD ** -0.5
BT = SEQ // P
GI = P // HEADS
GROUPS = SEQ // GI
TG = P // GI
SLOTS = 4
OC = HEADS // 4
P_SCALE = 4096.0
A_MAX = 16384.0
V_MAX = 16384.0
F16 = mybir.dt.float16
F32R = mybir.dt.float32r


def talking_heads(nc, g, x_dram, w_qkv, b_qkv, w_pre, w_post, w_post_all, w_out, b_out, cos, sin, same_token):
    with ExitStack() as ctx:
        sb = lambda n, s, d=F32: ctx.enter_context(nc.sbuf_tensor(f"at_{n}", s, d))
        ps = lambda n, s: ctx.enter_context(nc.psum_tensor(f"at_{n}", s, F32))
        sem = ctx.enter_context(stage_semaphores(nc, "at"))
        x_next = sb("x_next", [P, BT, DIM])
        x = sb("x", [P, BT, DIM])
        wqkv = sb("wqkv", [P, KC, 3 * DIM])
        wout = sb("wout", [P, OC, DIM])
        bqkv = sb("bqkv", [P, 3 * DIM])
        bout = sb("bout", [P, DIM])
        cost = sb("cos", [P, BT, HALF])
        sint = sb("sin", [P, BT, HALF])
        wpre = sb("wpre", [P, KC, HEADS])
        wpost16 = sb("wpost16", [P, HEADS])
        samet = sb("same_token", [P, P])
        wpost = sb("wpost", [P, HEADS, GI])
        xn = sb("xn", [P, BT, DIM])
        xnT = sb("xnT", [P, 2, KC, P])
        stats = sb("stats", [P, BT, 6])
        aggr = sb("aggr", [P, BT, 2])
        var_eps = sb("var_eps", [P, BT])
        rstd = sb("rstd", [P, BT])
        minus_half = sb("minus_half", [P, BT])
        qkv = sb("qkv", [P, 3 * DIM])
        rope_a = sb("rope_a", [P, 2 * HEADS, 2, HALF])
        rot = sb("rot", [P, 2 * HEADS, 2, HALF])
        qT = sb("qT", [P, KC, SEQ])
        k_hi = sb("k_hi", [P, KC, SEQ], F32R)
        k_lo = sb("k_lo", [P, KC, SEQ], F32R)
        k_bf = sb("k_bf", [P, KC, SEQ], BF16)
        v_parts = sb("v_parts", [P, BT, HEADS, 2, HD], F16)
        ones = sb("ones", [P, P])
        vmax = sb("vmax", [P, 4])
        q_full = sb("q_full", [P, KC, HEADS, GI])
        q_hi = sb("q_hi", [P, SLOTS, KC, HEADS * GI], F32R)
        q_lo = sb("q_lo", [P, SLOTS, KC, HEADS * GI], BF16)
        nmax = sb("nmax", [P, SLOTS])
        nbias = sb("nbias", [P, SLOTS])
        psum_row = sb("prob_sum", [P, SLOTS])
        rsum = sb("rsum", [P, SLOTS])
        wp_hi = sb("wp_hi", [P, SLOTS, P], F16)
        wp_lo = sb("wp_lo", [P, SLOTS, P], F16)
        p_full = sb("p_full", [P, SLOTS, SEQ])
        wsquare = p_full[:, 0:KC, 0:DIM]
        wabs = p_full[:, KC, 0:HEADS * HEADS]
        p_hi = sb("p_hi", [P, SLOTS, SEQ], F16)
        p_lo = sb("p_lo", [P, SLOTS, SEQ], F16)
        a_parts = sb("a_parts", [P, BT, HEADS, 2, P], F16)
        a_hi, a_lo = a_parts[:, :, :, 0, :], a_parts[:, :, :, 1, :]
        oT = sb("oT", [P, BT, OC, P])
        wmax = sb("wmax", [P, 1])
        unscale = sb("unscale", [P, 1])
        rescale = sb("rescale", [P, 1])

        psL = ps("logits", [P, 2, SEQ])
        psM = ps("mixed", [P, 2, 512])
        psO = ps("o", [P, OC, 2, P])
        psT = psO[:, 0:2, :, :].rearrange("p c s i -> p (c s i)")

        const_in = sem("const_in")
        const_ready = sem("const_ready")
        norms_done = sem("norms_done")
        norm_ready = sem("norm_ready")
        root_ready = sem("root_ready")
        x_next_in = sem("x_next_in")
        x_in = sem("x_in")
        x_out = sem("x_out")
        stats_ready = sem("stats_ready")
        stats_waited = sem("stats_waited")
        aggr_ready = sem("aggr_ready")
        var_ready = sem("var_ready")
        rstd_ready = sem("rstd_ready")
        xn_ready = sem("xn_ready")
        xn_transposed = sem("xn_transposed")
        xnT_ready = sem("xnT_ready")
        qkv_done = sem("qkv_done")
        qkv_ready = sem("qkv_ready")
        v_waited = sem("v_waited")
        v_part = sem("v_part")
        v_ready = sem("v_ready")
        rope_ready = sem("rope_ready")
        rot_ready = sem("rot_ready")
        rot_read = sem("rot_read")
        rot_transposed = sem("rot_transposed")
        qk_copied = sem("qk_copied")
        qk_ready = sem("qk_ready")
        q_full_done = sem("q_full_done")
        q_hi_done = sem("q_hi_done")
        q_built = sem("q_built")
        logits_done = sem("logits_done")
        max_done = sem("max_done")
        bias_done = sem("bias_done")
        exp_done = sem("exp_done")
        rsum_done = sem("rsum_done")
        wp_part = sem("wp_part")
        wp_ready = sem("wp_ready")
        p_hi_done = sem("p_hi_done")
        p_lo_done = sem("p_lo_done")
        mixed_done = sem("mixed_done")
        a_hi_done = sem("a_hi_done")
        a_lo_done = sem("a_lo_done")
        o_done = sem("o_done")
        oT_part = sem("oT_part")
        oT_ready = sem("oT_ready")
        out_done = sem("out_done")
        biased = sem("biased")
        x_ready = sem("x_ready")
        block = ctx.enter_context(nc.Block())

        made = lambda n: n + 1 + SLOTS
        free = lambda n: n + 1
        made2 = lambda n: n + 1 + 2
        free2 = lambda n: n + 1
        CONSTS = 11

        def groups(eng, b, step):
            def quad(t, q, left=SLOTS, after_tile=False):
                for slot in range(SLOTS):
                    step(b, t, q * SLOTS + slot, slot, min(left + SLOTS - 1 - slot, SLOTS), after_tile)

            quads = TG // SLOTS
            quad(0, 0)
            with eng.Fori(1, quads) as q:
                quad(0, q)
            with eng.Fori(1, BT - 1) as t:
                quad(t, 0, after_tile=True)
                with eng.Fori(1, quads) as q:
                    quad(t, q)
            quad(BT - 1, 0, after_tile=True)
            with eng.Fori(1, quads - 1) as q:
                quad(BT - 1, q)
            quad(BT - 1, quads - 1, left=0)

        @block.sync
        def _(sp):
            rows_of = lambda b: x_dram[b * SEQ:(b + 1) * SEQ, :].rearrange("(t p) d -> p t d", p=P)
            sp.dma_start(x_next[:, :, :], rows_of(0)).then_inc(x_next_in, 16)
            bc = lambda a: a.partition_broadcast(P)
            for dst, src in ((wqkv[:, :, :], w_qkv.rearrange("(c p) d -> p c d", p=P)),
                             (wout[:, :, :], w_out),
                             (bqkv[:, :], bc(b_qkv)), (bout[:, :], bc(b_out)),
                             (cost[:, :, :], cos.rearrange("(t p) f -> p t f", p=P)),
                             (sint[:, :, :], sin.rearrange("(t p) f -> p t f", p=P)),
                             (wpre[:, 0, :], w_pre[0:P, :]), (wpre[:, 1, :], w_pre[P:DIM, :]),
                             (wpost16[:, :], w_post), (samet[:, :], same_token),
                             (wabs, bc(w_post_all))):
                sp.dma_start(dst, src).then_inc(const_in, 16)
            for b in range(BATCH):
                rows = rows_of(b)
                sp.dma_start(x[:, :, :], rows).then_inc(x_in, 16)
                sp.wait_ge(xn_ready, (b + 1) * BT)
                sp.dma_start(x_next[:, :, :], rows_of((b + 1) % BATCH)).then_inc(x_next_in, 16)
                sp.wait_ge(x_ready, (b + 1) * BT + 1)
                sp.dma_start(rows, x[:, :, :]).then_inc(x_out, 16)
                sp.wait_ge(x_out, (b + 1) * 16)

        @block.vector
        def _(dve):
            for sem_ in (q_hi_done, max_done, bias_done, rsum_done, wp_part, wp_ready):
                dve.sem_inc(sem_, SLOTS)
            dve.sem_inc(a_lo_done, 2)
            dve.sem_inc(rot_read, 1)
            dve.sem_inc(x_ready, 1)
            dve.sem_inc(oT_ready, 1)
            def layer_norm(b):
                dve.wait_ge(x_next_in, (b + 1) * 16)
                for t in range(BT):
                    nc.vector.bn_stats(stats[:, t, :], x_next[:, t, :]).then_inc(stats_ready, 1)
                dve.wait_ge(stats_ready, (b + 1) * BT)
                dve.sem_inc(stats_waited, 1)
                for t in range(BT):
                    nc.vector.bn_aggr(aggr[:, t, :], stats[:, t, :]).then_inc(aggr_ready, 1)
                dve.wait_ge(aggr_ready, (b + 1) * BT)
                nc.vector.tensor_scalar(var_eps[:, :], aggr[:, :, 1], LN_EPS, None, ALU.add).then_inc(var_ready, 1)
                dve.wait_ge(rstd_ready, b + 1)
                for t in range(BT):
                    nc.vector.tensor_scalar(xn[:, t, :], x_next[:, t, :], aggr[:, t, 0:1], rstd[:, t:t + 1],
                                            ALU.subtract, ALU.mult).then_inc(xn_ready, 1)

            nc.vector.memset(minus_half[:, :], -0.5).then_inc(const_ready, 1)
            layer_norm(0)
            dve.wait_ge(const_in, 16 * CONSTS)
            nc.vector.tensor_scalar(wpre[:, :, :], wpre[:, :, :], SCALE, None, ALU.mult).then_inc(const_ready, 1)
            nc.vector.tensor_tensor(wpost[:, :, :], wpost16[:, :].unsqueeze(2).broadcast_to([P, HEADS, GI]),
                                    samet[:, :].rearrange("p (g i) -> p g i", i=GI), ALU.mult).then_inc(const_ready, 1)
            nc.vector.memset(ones[:, :], 1.0).then_inc(const_ready, 1)
            nc.vector.memset(vmax[:, 3:4], 0.5).then_inc(const_ready, 1)
            nc.vector.tensor_reduce(wmax[:, :], wabs, AX_X, ALU.max, apply_absolute_value=True).then_inc(const_ready, 1)
            nc.vector.tensor_tensor(wsquare[:, :, :], wqkv[:, :, 2 * DIM:], wqkv[:, :, 2 * DIM:], ALU.mult).then_inc(const_ready, 1)
            nc.vector.tensor_reduce(vmax[:, 1:2], bqkv[:, 2 * DIM:], AX_X, ALU.max, apply_absolute_value=True).then_inc(const_ready, 1)
            dve.wait_ge(const_ready, 8)
            nc.vector.tensor_scalar(unscale[:, :], wmax[:, :], HEADS / A_MAX, 1e-30, ALU.mult, ALU.max).then_inc(const_ready, 1)
            dve.wait_ge(const_ready, 9)
            nc.vector.reciprocal(rescale[:, :], unscale[:, :]).then_inc(const_ready, 1)
            dve.wait_ge(const_ready, 10)
            nc.vector.tensor_scalar(wpost[:, :, :], wpost[:, :, :], rescale[:, 0:1], P_SCALE, ALU.mult, ALU.mult).then_inc(const_ready, 1)
            dve.wait_ge(norms_done, 1)
            nc.vector.tensor_reduce(vmax[:, 0:1], psM[:, 0, 0:DIM], AX_X, ALU.max).then_inc(norm_ready, 1)
            dve.wait_ge(root_ready, 1)
            nc.vector.tensor_scalar(vmax[:, 2:3], vmax[:, 2:3], DIM ** 0.5, vmax[:, 1:2], ALU.mult, ALU.add).then_inc(norm_ready, 1)
            dve.wait_ge(norm_ready, 2)
            nc.vector.tensor_scalar(vmax[:, 2:3], vmax[:, 2:3], 1 / V_MAX, 1e-30, ALU.mult, ALU.max).then_inc(norm_ready, 1)
            dve.wait_ge(norm_ready, 3)
            nc.vector.reciprocal(vmax[:, 0:1], vmax[:, 2:3]).then_inc(norm_ready, 1)
            nc.vector.tensor_tensor(unscale[:, :], unscale[:, :], vmax[:, 2:3], ALU.mult).then_inc(norm_ready, 1)
            dve.wait_ge(norm_ready, 5)
            nc.vector.tensor_scalar(wqkv[:, :, 2 * DIM:], wqkv[:, :, 2 * DIM:], vmax[:, 0:1], None, ALU.mult).then_inc(norm_ready, 1)
            nc.vector.tensor_scalar(bqkv[:, 2 * DIM:], bqkv[:, 2 * DIM:], vmax[:, 0:1], None, ALU.mult).then_inc(norm_ready, 1)
            dve.wait_ge(norm_ready, 7)

            def high_q(b, k, slot):
                src = qT[:, :, bass.ds(k * GI, GI)].unsqueeze(2).broadcast_to([P, KC, HEADS, GI])
                weights = wpre[:, :, :].unsqueeze(3).broadcast_to([P, KC, HEADS, GI])
                dve.wait_ge(logits_done, free(b * GROUPS + k))
                nc.vector.tensor_tensor(q_hi[:, slot].rearrange("p c (g i) -> p c g i", i=GI), src, weights, ALU.mult).then_inc(q_hi_done, 1)

            def row_max(n, slot):
                dve.wait_ge(logits_done, made(n))
                nc.vector.tensor_reduce(nmax[:, slot:slot + 1], psL[:, slot % 2, :], AX_X, ALU.max, negate=True).then_inc(max_done, 1)
                dve.wait_ge(max_done, made(n))
                nc.vector.tensor_scalar(nbias[:, slot:slot + 1], nmax[:, slot:slot + 1], math.log(P_SCALE), None, ALU.add).then_inc(bias_done, 1)

            def post_weights(n, slot):
                dve.wait_ge(exp_done, made(n))
                nc.vector.reciprocal(rsum[:, slot:slot + 1], psum_row[:, slot:slot + 1]).then_inc(rsum_done, 1)
                dve.wait_ge(rsum_done, made(n))
                dve.wait_ge(mixed_done, free(n) * 2)
                flat = wpost[:, :, :].rearrange("p g i -> p (g i)")
                nc.vector.tensor_scalar(wp_hi[:, slot, :], flat, rsum[:, slot:slot + 1], None, ALU.mult).then_inc(wp_part, 1)
                dve.wait_ge(wp_part, made(n))
                nc.vector.scalar_tensor_tensor(wp_lo[:, slot, :], flat, rsum[:, slot:slot + 1],
                                               wp_hi[:, slot, :], ALU.mult, ALU.subtract).then_inc(wp_ready, 1)

            def step(b, t, k, slot, left, after_tile):
                n = b * GROUPS + t * TG + k
                ahead = (slot + 2) % SLOTS
                if left >= 2:
                    row_max(n + 2, ahead)
                for half in range(2):
                    h = n * 2 + half
                    dve.wait_ge(a_hi_done, made2(h))
                    blocks = slice(half * 4, half * 4 + 4)
                    nc.vector.scalar_tensor_tensor(
                        a_lo[:, blocks, :, bass.ds(k * GI, GI)].rearrange("p j g i -> p (j g) i"),
                        psM[:, half, :].rearrange("p (j i) -> p j i", i=GI), 1 / P_SCALE,
                        a_hi[:, blocks, :, bass.ds(k * GI, GI)].rearrange("p j g i -> p (j g) i"),
                        ALU.mult, ALU.subtract).then_inc(a_lo_done, 1)
                if left >= SLOTS:
                    high_q(b, t * TG + k + SLOTS, slot)
                if left >= 2:
                    post_weights(n + 2, ahead)
                if after_tile and slot == 1:
                    add_o(b, t - 1)

            def add_o(b, t):
                dve.wait_ge(oT_part, b * BT + t + 1)
                into = oT[:, bass.ds(t, 1), :, :].rearrange("p a c i -> p (a c) i")
                nc.vector.scalar_tensor_tensor(into, psO[:, :, 1, :], unscale[:, 0:1], into, ALU.mult, ALU.add).then_inc(oT_ready, 1)

            with dve.Fori(0, BATCH) as b:
                def k_low(t):
                    m = b * BT + t
                    dve.wait_ge(qk_copied, m + 1)
                    cols = slice(t * P, (t + 1) * P)
                    nc.vector.tensor_tensor(k_lo[:, :, cols], psT[:, 256:512].rearrange("p (c i) -> p c i", c=KC),
                                            k_hi[:, :, cols].bitcast(F32), ALU.subtract).then_inc(qk_ready, 1)

                for t in range(BT):
                    m = b * BT + t
                    dve.wait_ge(qkv_done, m + 1)
                    dve.wait_ge(v_ready, m + 1)
                    dve.wait_ge(rot_read, m + 1)
                    nc.vector.tensor_tensor(qkv[:, :], psL[:, t % 2, 0:3 * DIM], bqkv[:, :], ALU.add).then_inc(qkv_ready, 1)
                    dve.wait_ge(qkv_ready, m + 1)
                    qk = qkv[:, 0:2 * DIM].rearrange("p (h a f) -> p h a f", a=2, f=HALF)
                    c1 = cost[:, t, :].unsqueeze(1).broadcast_to([P, 2 * HEADS, HALF])
                    s1 = sint[:, t, :].unsqueeze(1).broadcast_to([P, 2 * HEADS, HALF])
                    nc.vector.tensor_tensor(rope_a[:, :, 0, :], qk[:, :, 1, :], s1, ALU.mult).then_inc(rope_ready, 1)
                    nc.vector.tensor_tensor(rope_a[:, :, 1, :], qk[:, :, 0, :], s1, ALU.mult).then_inc(rope_ready, 1)
                    dve.wait_ge(rot_transposed, m + 1)
                    nc.vector.tensor_tensor(rot[:, :, 0, :], qk[:, :, 0, :], c1, ALU.mult).then_inc(rope_ready, 1)
                    nc.vector.tensor_tensor(rot[:, :, 1, :], qk[:, :, 1, :], c1, ALU.mult).then_inc(rope_ready, 1)
                    dve.wait_ge(rope_ready, (m + 1) * 4)
                    nc.vector.tensor_tensor(rot[:, :, 0, :], rot[:, :, 0, :], rope_a[:, :, 0, :], ALU.subtract).then_inc(rot_ready, 1)
                    nc.vector.tensor_tensor(rot[:, :, 1, :], rot[:, :, 1, :], rope_a[:, :, 1, :], ALU.add).then_inc(rot_ready, 1)
                    dve.wait_ge(rot_ready, (m + 1) * 2)
                    dve.sem_inc(rot_read, 1)
                    if t:
                        k_low(t - 1)
                    if t == 2:
                        for k in range(SLOTS):
                            high_q(b, k, k)
                k_low(BT - 1)
                for slot in range(2):
                    row_max(b * GROUPS + slot, slot)
                    post_weights(b * GROUPS + slot, slot)
                groups(dve, b, step)
                layer_norm(b + 1)
                add_o(b, BT - 1)
                dve.wait_ge(x_in, (b + 1) * 16)
                for t in range(BT):
                    m = b * BT + t
                    nc.vector.tensor_tensor(x[:, t, :], x[:, t, :], bout[:, :], ALU.add).then_inc(biased, 1)
                    dve.wait_ge(biased, m + 1)
                    dve.wait_ge(out_done, m + 1)
                    nc.vector.tensor_tensor(x[:, t, :], x[:, t, :], psL[:, t % 2, 0:DIM], ALU.add).then_inc(x_ready, 1)

        @block.gpsimd
        def _(pool):
            for sem_ in (q_built, p_lo_done):
                pool.sem_inc(sem_, SLOTS)
            pool.sem_inc(v_ready, 1)

            def rsqrt(b):
                pool.wait_ge(var_ready, b + 1)
                nc.gpsimd.tensor_tensor(rstd[:, :], var_eps[:, :], minus_half[:, :], ALU.pow).then_inc(rstd_ready, 1)

            pool.wait_ge(const_ready, 1)
            rsqrt(0)
            pool.wait_ge(const_ready, 11)
            pool.wait_ge(norm_ready, 1)
            nc.gpsimd.tensor_tensor(vmax[:, 2:3], vmax[:, 0:1], vmax[:, 3:4], ALU.pow).then_inc(root_ready, 1)
            weights = wpre[:, :, :].unsqueeze(3).broadcast_to([P, KC, HEADS, GI])

            def build_q(b, k, slot):
                n = b * GROUPS + k
                src = qT[:, :, bass.ds(k * GI, GI)].unsqueeze(2).broadcast_to([P, KC, HEADS, GI])
                pool.wait_ge(q_built, n + SLOTS)
                nc.gpsimd.tensor_tensor(q_full[:, :, :, :], src, weights, ALU.mult).then_inc(q_full_done, 1)
                pool.wait_ge(q_full_done, n + 1)
                pool.wait_ge(q_hi_done, made(n))
                nc.gpsimd.tensor_tensor(q_lo[:, slot], q_full[:, :, :, :].rearrange("p c g i -> p c (g i)"),
                                        q_hi[:, slot].bitcast(F32), ALU.subtract).then_inc(q_built, 1)

            def low_p(n, slot):
                pool.wait_ge(p_hi_done, made(n))
                nc.gpsimd.tensor_tensor(p_lo[:, slot, :], p_full[:, slot, :], p_hi[:, slot, :], ALU.subtract).then_inc(p_lo_done, 1)

            def step(b, t, k, slot, left, after_tile):
                low_p(b * GROUPS + t * TG + k, slot)
                if left >= SLOTS - 1:
                    build_q(b, t * TG + k + SLOTS - 1, (slot - 1) % SLOTS)

            with pool.Fori(0, BATCH) as b:
                for t in range(BT):
                    m = b * BT + t
                    v = qkv[:, 2 * DIM:3 * DIM].rearrange("p (h f) -> p h f", f=HD)
                    pool.wait_ge(qkv_ready, m + 1)
                    pool.sem_inc(v_waited, 1)
                    nc.gpsimd.tensor_copy(v_parts[:, t, :, 0, :], v).then_inc(v_part, 1)
                    pool.wait_ge(v_part, m + 1)
                    nc.gpsimd.tensor_tensor(v_parts[:, t, :, 1, :], v, v_parts[:, t, :, 0, :], ALU.subtract).then_inc(v_ready, 1)
                    if 4 <= t < 4 + SLOTS - 1:
                        pool.wait_ge(qk_ready, b * BT + 1)
                        build_q(b, t - 4, t - 4)
                groups(pool, b, step)
                rsqrt(b + 1)

        @block.scalar
        def _(act):
            for sem_ in (exp_done, p_hi_done):
                act.sem_inc(sem_, SLOTS)
            act.sem_inc(a_hi_done, 2)

            def softmax_exp(n, slot):
                act.wait_ge(bias_done, made(n))
                act.wait_ge(p_lo_done, free(n))
                act.wait_ge(rsum_done, free(n))
                nc.scalar.activation(p_full[:, slot, :], psL[:, slot % 2, :], ACT.Exp, bias=nbias[:, slot:slot + 1],
                                     accum_out=psum_row[:, slot:slot + 1]).then_inc(exp_done, 1)

            def high_p(n, slot):
                act.wait_ge(exp_done, made(n))
                act.wait_ge(mixed_done, free(n) * 2)
                nc.scalar.copy(p_hi[:, slot, :], p_full[:, slot, :]).then_inc(p_hi_done, 1)

            def high_a(n, k, half):
                act.wait_ge(mixed_done, n * 2 + half + 1 + 2 * SLOTS)
                nc.scalar.mul(a_hi[:, half * 4:half * 4 + 4, :, bass.ds(k * GI, GI)],
                              psM[:, half, :].rearrange("p (j g i) -> p j g i", j=4, g=HEADS), 1 / P_SCALE).then_inc(a_hi_done, 1)

            def copy_o(b, t):
                act.wait_ge(o_done, b * BT + t + 1)
                nc.scalar.activation(oT[:, bass.ds(t, 1), :, :].rearrange("p a c i -> p (a c) i"),
                                     psO[:, :, 0, :], ACT.Copy, scale=unscale[:, 0:1]).then_inc(oT_part, 1)

            def step(b, t, k, slot, left, after_tile):
                n = b * GROUPS + t * TG + k
                high_a(n, k, 0)
                high_a(n, k, 1)
                if left >= 2:
                    softmax_exp(n + 2, (slot + 2) % SLOTS)
                    high_p(n + 2, (slot + 2) % SLOTS)
                if after_tile and slot == 0:
                    copy_o(b, t - 1)

            act.wait_ge(norm_ready, 7)
            with act.Fori(0, BATCH) as b:
                def qk_copy(t):
                    m = b * BT + t
                    act.wait_ge(rot_transposed, m + 2)
                    cols = slice(t * P, (t + 1) * P)
                    nc.scalar.copy(qT[:, :, cols], psT[:, 0:256].rearrange("p (c i) -> p c i", c=KC))
                    kps = psT[:, 256:512].rearrange("p (c i) -> p c i", c=KC)
                    nc.scalar.copy(k_bf[:, :, cols], kps)
                    nc.scalar.copy(k_hi[:, :, cols], kps).then_inc(qk_copied, 1)

                def xn_copy(t):
                    m = b * BT + t
                    act.wait_ge(xn_transposed, m + 1)
                    nc.scalar.copy(xnT[:, t % 2], psM[:, t % 2, 0:DIM].rearrange("p (c i) -> p c i", c=KC)).then_inc(xnT_ready, 1)

                xn_copy(0)
                for t in range(BT):
                    if t + 1 < BT:
                        xn_copy(t + 1)
                    if t:
                        qk_copy(t - 1)
                qk_copy(BT - 1)
                for slot in range(2):
                    softmax_exp(b * GROUPS + slot, slot)
                    high_p(b * GROUPS + slot, slot)
                groups(act, b, step)
                copy_o(b, BT - 1)

        @block.tensor
        def _(pe):
            pe.sem_inc(logits_done, SLOTS)
            pe.sem_inc(mixed_done, 2 * SLOTS)
            pe.sem_inc(rot_transposed, 1)
            pe.wait_ge(const_ready, 8)
            for c in range(KC):
                last = nc.tensor.matmul(psM[:, 0, 0:DIM], ones[:, :], wsquare[:, c, :], start=c == 0, stop=c == KC - 1)
            last.then_inc(norms_done, 1)
            pe.wait_ge(norm_ready, 7)

            def logits(n, slot):
                pe.wait_ge(q_built, made(n))
                pe.wait_ge(exp_done, n - 1 + SLOTS)
                for half in range(2):
                    keys = slice(half * 512, half * 512 + 512)
                    k = 0
                    for c in range(KC):
                        for left, right in ((q_hi, k_hi), (q_hi, k_lo), (q_lo, k_bf)):
                            last = nc.tensor.matmul(psL[:, slot % 2, keys], left[:, slot, c, :], right[:, c, keys], start=k == 0, stop=k == 5)
                            k += 1
                last.then_inc(logits_done, 1)

            def mix(n, slot):
                pe.wait_ge(wp_ready, made(n))
                pe.wait_ge(p_lo_done, made(n))
                for half in range(2):
                    pe.wait_ge(a_lo_done, free2(n * 2 + half))
                    for j in range(4):
                        keys = slice(half * 512 + j * P, half * 512 + (j + 1) * P)
                        out = psM[:, half, j * P:(j + 1) * P]
                        nc.tensor.matmul(out, p_hi[:, slot, keys], wp_hi[:, slot, :], start=True, stop=False)
                        nc.tensor.matmul(out, p_hi[:, slot, keys], wp_lo[:, slot, :], start=False, stop=False)
                        last = nc.tensor.matmul(out, p_lo[:, slot, keys], wp_hi[:, slot, :], start=False, stop=True)
                    last.then_inc(mixed_done, 1)

            def attend(b, t):
                m = b * BT + t
                pe.wait_ge(a_lo_done, made2((m + 1) * TG * 2 - 1))
                pe.wait_ge(oT_ready, m + 1)
                for c in range(OC):
                    for j in range(BT):
                        for q in range(4):
                            h = c * 4 + q
                            last = nc.tensor.matmul(psO[q * 32:(q + 1) * 32, c, :, :].rearrange("p s i -> p (s i)"), v_parts[:, j, h].rearrange("p s f -> p (s f)"),
                                                    a_parts[:, j, h, :, :].rearrange("p s i -> p (s i)"), start=j == 0, stop=j == BT - 1, skip_group_check=True)
                last.then_inc(o_done, 1)

            def step(b, t, k, slot, left, after_tile):
                n = b * GROUPS + t * TG + k
                if left >= 2:
                    logits(n + 2, (slot + 2) % SLOTS)
                if after_tile and slot == 0:
                    attend(b, t - 1)
                mix(n, slot)

            with pe.Fori(0, BATCH) as b:
                def qk_transpose(t):
                    m = b * BT + t
                    pe.wait_ge(rot_ready, (m + 1) * 2)
                    if t:
                        pe.wait_ge(qk_ready, m)
                    else:
                        pe.wait_ge(xn_ready, b * BT + 1)
                    flat = rot[:, :, :, :].rearrange("p h a f -> p (h a f)")
                    for c in range(2 * KC):
                        last = nc.tensor.transpose(psT[:, c * P:(c + 1) * P], flat[:, c * P:(c + 1) * P], g.ident[:, :])
                    last.then_inc(rot_transposed, 1)

                def xn_transpose(t):
                    m = b * BT + t
                    pe.wait_ge(xn_ready, m + 1)
                    if t >= 2:
                        pe.wait_ge(xnT_ready, m - 1)
                    for c in range(KC):
                        last = nc.tensor.transpose(psM[:, t % 2, c * P:(c + 1) * P], xn[:, t, c * P:(c + 1) * P], g.ident[:, :])
                    last.then_inc(xn_transposed, 1)

                pe.wait_ge(x_ready, b * BT + 1)
                xn_transpose(0)
                for t in range(BT):
                    m = b * BT + t
                    if t + 1 < BT:
                        xn_transpose(t + 1)
                    pe.wait_ge(xnT_ready, m + 1)
                    if t >= 2:
                        pe.wait_ge(qkv_ready, m - 1)
                    for lo, hi in ((0, 512), (512, 768)):
                        for c in range(KC):
                            last = nc.tensor.matmul(psL[:, t % 2, lo:hi], xnT[:, t % 2, c, :], wqkv[:, c, lo:hi], start=c == 0, stop=c == KC - 1)
                    last.then_inc(qkv_done, 1)
                    if t:
                        qk_transpose(t - 1)
                qk_transpose(BT - 1)
                pe.wait_ge(qk_ready, (b + 1) * BT)
                pe.wait_ge(v_ready, (b + 1) * BT + 1)
                for slot in range(2):
                    logits(b * GROUPS + slot, slot)
                groups(pe, b, step)
                attend(b, BT - 1)
                for t in range(BT):
                    m = b * BT + t
                    pe.wait_ge(oT_ready, m + 2)
                    if t >= 2:
                        pe.wait_ge(x_ready, m)
                    for c in range(OC):
                        last = nc.tensor.matmul(psL[:, t % 2, 0:DIM], oT[:, t, c, :], wout[:, c, :], start=c == 0, stop=c == OC - 1)
                    last.then_inc(out_done, 1)


FEAT = 64
PAIRS = HEADS // 2
V1 = HD + 1
HPC = P // HD
QUAD = 4
Z_EPS = 1e-8


def linear_attention(nc, g, name, w_qkv, proj, w_out, b_out):
    with ExitStack() as ctx:
        sb = lambda n, s, d=F32: ctx.enter_context(nc.sbuf_tensor(f"{name}_{n}", s, d))
        ps = lambda n, s: ctx.enter_context(nc.psum_tensor(f"{name}_{n}", s, F32))
        sem = ctx.enter_context(stage_semaphores(nc, name))
        HB = SEQ // CHUNK
        FS = 4
        GROUP = QUAD * FEAT
        wqkv = sb("wqkv", [P, KC, 3 * DIM])
        wout = sb("wout", [P, KC, DIM])
        bout = sb("bout", [P, DIM])
        proj_diag = sb("proj_diag", [P, KC, HPC * FEAT])
        xn = sb("xn", [P, BT, DIM])
        xT = sb("xT", [P, KC, CHUNK])
        qT = sb("qT", [P, KC, SEQ])
        kT = sb("kT", [P, KC, SEQ])
        v_one = sb("v_one", [P, BT, HEADS, V1])
        negative = sb("negative", [P, FS, CHUNK])
        exped = sb("exped", [P, FS, CHUNK])
        k_feat = sb("k_feat", [P, BT, HEADS * FEAT])
        q_feat = sb("q_feat", [P, PAIRS, SEQ])
        kvT = sb("kvT", [P, HEADS // QUAD, GROUP])
        kv = sb("kv", [P, PAIRS, 2 * HD])
        k_sum = sb("k_sum", [P, PAIRS, 2 * HD])
        z = sb("z", [P, 2, CHUNK])
        oT = sb("oT", [P, KC, SEQ])
        delta = sb("delta", [P, 2, DIM])
        psT = ps("psT", [P, KC, CHUNK])
        psQ = ps("psQ", [P, 2, CHUNK])
        psF = ps("psF", [P, FS, CHUNK])

        const_in = sem("const_in")
        diag_zero = sem("diag_zero")
        diag_in = sem("diag_in")
        ones_set = sem("ones_set")
        xn_ready = sem("xn_ready")
        transposed = sem("transposed")
        psT_free = sem("psT_free")
        xT_ready = sem("xT_ready")
        proj_done = sem("proj_done")
        out_done = sem("out_done")
        slot_free = [sem(f"slot_free{s}") for s in range(2)]
        qkv_ready = sem("qkv_ready")
        feat_done = sem("feat_done")
        psF_free = sem("psF_free")
        neg_act = sem("neg_act")
        neg_dve = sem("neg_dve")
        exp_ready = sem("exp_ready")
        kvT_done = sem("kvT_done")
        kvT_ready = sem("kvT_ready")
        kv_transposed = sem("kv_transposed")
        kv_ready = sem("kv_ready")
        attended = sem("attended")
        z_sum = sem("z_sum")
        z_ready = sem("z_ready")
        oT_ready = sem("oT_ready")
        delta_ready = sem("delta_ready")
        delta_free = sem("delta_free")
        block = ctx.enter_context(nc.Block())
        norm = TokenNorm(nc, g, sem)
        K_UNITS = BT * KC
        UNITS = K_UNITS + HB * PAIRS
        O_UNITS = HB * KC
        F_USES = UNITS + 2 * O_UNITS
        QKV_UNITS = HB * 6
        SLOT_USES = (QKV_UNITS + 2 + BT) // 2
        T_USES = HB + 1

        @block.sync
        def _(sp):
            sp.dma_start(wqkv[:, :, :], w_qkv.rearrange("(c p) d -> p c d", p=P)).then_inc(const_in, 16)
            sp.dma_start(wout[:, :, :], w_out.rearrange("(c p) d -> p c d", p=P)).then_inc(const_in, 16)
            sp.dma_start(bout[:, :], b_out.partition_broadcast(P)).then_inc(const_in, 16)
            sp.wait_ge(diag_zero, 1)
            for h in range(HEADS):
                c, m = h // HPC, h % HPC
                sp.dma_start(proj_diag[m * HD:(m + 1) * HD, c, m * FEAT:(m + 1) * FEAT], proj[h]).then_inc(diag_in, 16)

        def sequences(eng, body):
            with eng.Fori(0, BATCH - 1) as b:
                body(b, True)
            body(BATCH - 1, False)

        on_act = lambda u: u % 2 == 0

        @block.vector
        def _(dve):
            def layer_norm(b):
                for k in range(BT):
                    t = b * BT + k
                    last = nc.vector.tensor_scalar(
                        xn[:, k, :], g.x[:, bass.ds(t, 1), :].rearrange("p a d -> p (a d)"),
                        g.aggr[:, bass.ds(t, 1), 0], g.rstd[:, bass.ds(t, 1)], ALU.subtract, ALU.mult)
                    if k % CT == CT - 1:
                        last.then_inc(xn_ready, 1)

            def negative_part(b, u):
                if on_act(u):
                    return
                dve.wait_ge(feat_done, b * UNITS + (u + 1))
                dve.wait_ge(exp_ready, b * UNITS + (u + 1))
                nc.vector.tensor_scalar(negative[:, u % FS, :], psF[:, u % FS, :], 0.0, None, ALU.min).then_inc(neg_dve, 1)

            def feature(b, u):
                if u < K_UNITS:
                    into = k_feat[:, u // KC, (u % KC) * CHUNK:(u % KC + 1) * CHUNK]
                else:
                    h, pair = divmod(u - K_UNITS, PAIRS)
                    into = q_feat[:, pair, h * CHUNK:(h + 1) * CHUNK]
                dve.wait_ge(exp_ready, b * UNITS + (u + 1 + FS))
                nc.vector.scalar_tensor_tensor(into, psF[:, u % FS, :], 0.0, exped[:, u % FS, :], ALU.max, ALU.add).then_inc(psF_free, 1)

            def normalise(b, o):
                n = b * O_UNITS + o
                h, c = divmod(o, KC)
                first = (UNITS + 2 * o) % FS
                dve.wait_ge(z_sum, n + 1)
                nc.vector.reciprocal(z[:, o % 2, :], z[:, o % 2, :]).then_inc(z_ready, 1)
                dve.wait_ge(z_ready, n + 1)
                dve.wait_ge(attended, 2 * n + 2)
                nc.vector.tensor_tensor(oT[:, c, h * CHUNK:(h + 1) * CHUNK], psF[:, first, :], z[:, o % 2, :], ALU.mult).then_inc(oT_ready, 1)
                dve.wait_ge(oT_ready, n + 1)
                dve.sem_inc(psF_free, 2)

            def add_bias(b, t):
                n = b * BT + t
                dve.wait_ge(out_done, n + 1)
                dve.wait_ge(delta_free, n + 1)
                s = t % 2
                nc.vector.tensor_tensor(delta[:, t % 2], psQ[:, s, 0:DIM], bout[:, :], ALU.add).then_inc(delta_ready, 1)
                dve.wait_ge(delta_ready, n + 1)
                dve.sem_inc(slot_free[s], 1)

            dve.sem_inc(psF_free, FS)
            nc.vector.memset(proj_diag[:, :, :], 0.0).then_inc(diag_zero, 1)
            nc.vector.memset(v_one[:, :, :, HD:V1], 1.0).then_inc(ones_set, 1)
            nc.vector.memset(kv[:, :, :], 0.0).then_inc(ones_set, 1)
            nc.vector.memset(k_sum[:, :, :], 0.0).then_inc(ones_set, 1)
            norm.statistics(dve)
            layer_norm(0)
            dve.wait_ge(const_in, 16 * 3)

            def body(b, more):
                negative_part(b, 0)
                for u in range(UNITS):
                    if u == K_UNITS and more:
                        layer_norm(b + 1)
                    if u + 1 < UNITS:
                        negative_part(b, u + 1)
                    feature(b, u)
                for o in range(O_UNITS):
                    normalise(b, o)
                for t in range(BT):
                    add_bias(b, t)

            sequences(dve, body)

        @block.gpsimd
        def _(pool):
            pool.sem_inc(delta_free, 2)
            norm.roots(pool)
            with pool.Fori(0, BATCH) as b:
                for t in range(BT):
                    n = b * BT + t
                    pool.wait_ge(delta_ready, n + 1)
                    xs = g.x[:, bass.ds(n, 1), :].rearrange("p a d -> p (a d)")
                    nc.gpsimd.tensor_tensor(xs, xs, delta[:, t % 2], ALU.add).then_inc(delta_free, 1)

        @block.scalar
        def _(act):
            act.sem_inc(psT_free, 1)
            act.sem_inc(slot_free[0], 1)
            act.sem_inc(slot_free[1], 1)
            act.sem_inc(exp_ready, FS)
            act.wait_ge(ones_set, 3)

            def copy_kvT(b, half):
                act.wait_ge(kvT_done, b * 2 + (half + 1))
                nc.scalar.copy(kvT[0:QUAD * V1, 2 * half:2 * half + 2, :], psQ[0:QUAD * V1, half, :].rearrange("p (g f) -> p g f", g=2)).then_inc(kvT_ready, 1)
                act.wait_ge(kvT_ready, b * 2 + (half + 1))
                act.sem_inc(slot_free[half], 1)

            def copy_qkv(b, h):
                act.wait_ge(transposed, b * HB + (h + 1))
                nc.scalar.copy(xT[:, :, :], psT[:, :, :]).then_inc(xT_ready, 1)
                act.wait_ge(xT_ready, b * HB + (h + 1))
                act.sem_inc(psT_free, 1)
                for k in range(6):
                    u = h * 6 + k
                    act.wait_ge(proj_done, b * QKV_UNITS + (u + 1))
                    if k < 2 * KC:
                        into = (qT if k < KC else kT)[:, k % KC, h * CHUNK:(h + 1) * CHUNK]
                        source = psQ[:, u % 2, :]
                    else:
                        t = h * CT + (k - 2 * KC) * 2
                        into = v_one[:, t:t + 2, :, 0:HD]
                        source = psQ[:, u % 2, :].rearrange("p (t h d) -> p t h d", t=2, d=HD)
                    nc.scalar.copy(into, source).then_inc(qkv_ready, 1)
                    act.wait_ge(qkv_ready, b * QKV_UNITS + (u + 1))
                    act.sem_inc(slot_free[u % 2], 1)

            def copy_kv(b):
                act.wait_ge(kv_transposed, b + 1)
                for m in range(2):
                    rows, cols = slice(m * FEAT, (m + 1) * FEAT), slice(m * HD, (m + 1) * HD)
                    for k in range(2):
                        lo = (2 * k + m) * V1
                        source = psT[rows, :, 0:4 * QUAD * V1].rearrange("p a (j v) -> p a j v", v=QUAD * V1)[:, :, k::2, :]
                        pick = lambda a: a[rows, :, cols].rearrange("p (a j) v -> p a j v", a=2)[:, :, k::2, :]
                        nc.scalar.copy(pick(kv), source[:, :, :, lo:lo + HD]).then_inc(kv_ready, 1)
                        nc.scalar.copy(pick(k_sum), source[:, :, :, lo + HD:lo + V1].broadcast_to([FEAT, 2, 2, HD])).then_inc(kv_ready, 1)
                act.wait_ge(kv_ready, b * 8 + 8)
                act.sem_inc(psT_free, 1)

            def body(b, more):
                half_units = UNITS // 2
                for u in range(UNITS):
                    if on_act(u):
                        act.wait_ge(feat_done, b * UNITS + (u + 1))
                        act.wait_ge(exp_ready, b * UNITS + (u + 1))
                        nc.scalar.activation(negative[:, u % FS, :], psF[:, u % FS, :], ACT.Relu, scale=-1.0).then_inc(neg_act, 1)
                        act.wait_ge(neg_act, b * half_units + (u // 2 + 1))
                    else:
                        act.wait_ge(neg_dve, b * half_units + (u // 2 + 1))
                    act.wait_ge(psF_free, b * F_USES + (u + 1))
                    nc.scalar.activation(exped[:, u % FS, :], negative[:, u % FS, :], ACT.Exp, scale=-1.0 if on_act(u) else 1.0).then_inc(exp_ready, 1)
                    if u == K_UNITS + 11:
                        copy_kvT(b, 0)
                copy_kvT(b, 1)
                copy_kv(b)
                for o in range(O_UNITS):
                    n = b * O_UNITS + o
                    act.wait_ge(attended, 2 * n + 1)
                    nc.scalar.activation(z[:, o % 2, :], psF[:, (UNITS + 2 * o + 1) % FS, :], ACT.Copy, bias=Z_EPS).then_inc(z_sum, 1)
                    if o % KC == KC - 1 and more:
                        copy_qkv(b + 1, o // KC)

            for h in range(HB):
                copy_qkv(0, h)
            sequences(act, body)

        @block.tensor
        def _(pe):
            def sums(b, group, used):
                if group % 2 == 0:
                    pe.wait_ge(slot_free[group // 2], used + 1)
                if group == 0:
                    pe.wait_ge(psF_free, b * F_USES + (K_UNITS + FS))
                for t in range(BT):
                    last = nc.tensor.matmul(psQ[0:QUAD * V1, group // 2, (group % 2) * GROUP:(group % 2 + 1) * GROUP],
                                            v_one[:, t, group * QUAD:(group + 1) * QUAD, :].rearrange("p h v -> p (h v)"),
                                            k_feat[:, t, group * GROUP:(group + 1) * GROUP], start=t == 0, stop=t == BT - 1)
                if group % 2 == 1:
                    last.then_inc(kvT_done, 1)

            def qkv(b, h, used):
                n = b * HB + h
                pe.wait_ge(xn_ready, n + 1)
                pe.wait_ge(psT_free, b * T_USES + (h + 1))
                for t in range(CT):
                    for c in range(KC):
                        last = nc.tensor.transpose(psT[:, c, t * P:(t + 1) * P], xn[:, h * CT + t, c * P:(c + 1) * P], g.ident[:, :])
                last.then_inc(transposed, 1)
                pe.wait_ge(xT_ready, n + 1)
                for k in range(6):
                    u = h * 6 + k
                    pe.wait_ge(slot_free[u % 2], used + (u // 2 + 1))
                    if k < 2 * KC:
                        for c in range(KC):
                            last = nc.tensor.matmul(psQ[:, u % 2, :], wqkv[:, c, k * P:(k + 1) * P], xT[:, c, :], start=c == 0, stop=c == KC - 1)
                    else:
                        for m in range(2):
                            t = (k - 2 * KC) * 2 + m
                            for c in range(KC):
                                last = nc.tensor.matmul(psQ[:, u % 2, m * DIM:(m + 1) * DIM], xT[:, c, t * P:(t + 1) * P], wqkv[:, c, 2 * DIM:3 * DIM], start=c == 0, stop=c == KC - 1)
                    last.then_inc(proj_done, 1)

            def body(b, more):
                used = b * SLOT_USES + QKV_UNITS // 2
                pe.wait_ge(qkv_ready, b * QKV_UNITS + QKV_UNITS)
                for u in range(UNITS):
                    pe.wait_ge(psF_free, b * F_USES + (u + 1))
                    if u < K_UNITS:
                        t, c = divmod(u, KC)
                        nc.tensor.matmul(psF[:, u % FS, :], kT[:, c, t * P:(t + 1) * P], proj_diag[:, c, :], start=True, stop=True).then_inc(feat_done, 1)
                    else:
                        h, pair = divmod(u - K_UNITS, PAIRS)
                        c, m = divmod(pair, PAIRS // KC)
                        nc.tensor.matmul(psF[:, u % FS, :], proj_diag[:, c, m * P:(m + 1) * P], qT[:, c, h * CHUNK:(h + 1) * CHUNK], start=True, stop=True).then_inc(feat_done, 1)
                    if u >= K_UNITS + 4 and (u - K_UNITS) % 3 == 0:
                        sums(b, (u - K_UNITS) // 3 - 2, used)
                pe.wait_ge(kvT_ready, b * 2 + 2)
                pe.wait_ge(psT_free, b * T_USES + T_USES)
                for pair in range(PAIRS):
                    group, k = divmod(pair, 2)
                    lo = (pair % 4) * QUAD * V1
                    last = nc.tensor.transpose(psT[:, pair // 4, lo:lo + QUAD * V1], kvT[0:QUAD * V1, group, k * P:(k + 1) * P], g.ident[0:QUAD * V1, 0:QUAD * V1])
                last.then_inc(kv_transposed, 1)
                pe.wait_ge(kv_ready, b * 8 + 8)
                for o in range(O_UNITS):
                    h, c = divmod(o, KC)
                    pe.wait_ge(psF_free, b * F_USES + (UNITS + 2 * o + 2 if o else UNITS + FS))
                    for part, left in ((1, k_sum), (0, kv)):
                        for q in range(4):
                            last = nc.tensor.matmul(psF[q * 32:(q + 1) * 32, (UNITS + 2 * o + part) % FS, :], left[:, c * 4 + q, :],
                                                    q_feat[:, c * 4 + q, h * CHUNK:(h + 1) * CHUNK], start=True, stop=True, skip_group_check=True)
                        last.then_inc(attended, 1)
                    if c == KC - 1 and more:
                        qkv(b + 1, h, used + 1)
                used = used + 1 + (QKV_UNITS // 2 if more else 0)
                for t in range(BT):
                    if t % CT == 0:
                        pe.wait_ge(oT_ready, b * O_UNITS + (t // CT + 1) * KC)
                    pe.wait_ge(slot_free[t % 2], used + (t // 2 + 1))
                    for c in range(KC):
                        last = nc.tensor.matmul(psQ[:, t % 2, 0:DIM], oT[:, c, t * P:(t + 1) * P], wout[:, c, :], start=c == 0, stop=c == KC - 1)
                    last.then_inc(out_done, 1)

            pe.wait_ge(const_in, 16 * 3)
            for h in range(HB):
                qkv(0, h, 0)
            pe.wait_ge(diag_in, 16 * HEADS)
            sequences(pe, body)


EXPERTS = 8
PER_GROUP = 2
FFN = int(DIM * 4 * (2.0 / 3.0))
FB = (FFN + P - 1) // P
FLAST = FFN - (FB - 1) * P
CAPACITY = TILES * P // EXPERTS
EC = CAPACITY // P
ROW = DIM + EXPERTS
BLOCKED = 4096.0


def route(nc, g, name, w_r, b_r, rows_dram, tri, seg, tok_p, tok_t, x_in, copies):
    with ExitStack() as ctx:
        sb = lambda n, s, d=F32: ctx.enter_context(nc.sbuf_tensor(f"{name}_{n}", s, d))
        ps = lambda n, s: ctx.enter_context(nc.psum_tensor(f"{name}_{n}", s, F32))
        sem = ctx.enter_context(stage_semaphores(nc, name))
        ET = EXPERTS * TILES
        wr = sb("wr", [P, KC, EXPERTS])
        br = sb("br", [P, EXPERTS])
        tri_sb = sb("tri", [P, P])
        tri_bf = sb("tri_bf", [P, P], BF16)
        ones_bf = sb("ones_bf", [P, P], BF16)
        segment = sb("segment", [P, 2 * ET])
        tokp = sb("tokp", [P, 1])
        tokt = sb("tokt", [P, EXPERTS, TILES])
        xT = sb("xT", [P, 2, 4, KC, P])
        by_expert = sb("by_expert", [EXPERTS, 2, 4, P])
        logit = sb("logit", [P, TILES, EXPERTS])
        top = sb("top", [P, TILES])
        prob = sb("prob", [P, EXPERTS, TILES])
        ge = sb("ge", [P, EXPERTS, TILES])
        count = sb("count", [P, EXPERTS], BF16)
        thr = sb("thr", [P, EXPERTS])
        base = sb("base", [P, EXPERTS])
        cand = sb("cand", [P, EXPERTS])
        kept = sb("kept", [P, EXPERTS])
        mask = sb("mask", [P, 2, EXPERTS, TILES], BF16)
        total = sb("total", [P, 2, EXPERTS, TILES])
        running = sb("running", [P, 2, EXPERTS, TILES])
        before = sb("before", [P, 2, EXPERTS, TILES])
        pos = sb("pos", [P, EXPERTS, TILES])
        hi = sb("hi", [P, EXPERTS, TILES])
        low, values = g.place, g.values
        psT = ps("psT", [P, 2, 4, KC, P])
        psR = ps("psR", [P, TILES, EXPERTS])
        psC = ps("psC", [P, 512])
        psE = ps("psE", [P, 2, 4, P])

        const_in = sem("const_in")
        const_ready = sem("const_ready")
        xn_ready = sem("xn_ready")
        transposed = sem("transposed")
        xT_ready = sem("xT_ready")
        routed = sem("routed")
        by_expert_done = sem("by_expert_done")
        by_expert_ready = sem("by_expert_ready")
        shifted = sem("shifted")
        exp_ready = sem("exp_ready")
        step_done = sem("dve_step")
        counted = sem("counted")
        summed = sem("summed")
        masks_ready = sem("masks_ready")
        prefix_done = sem("prefix_done")
        total_ready = sem("total_ready")
        rows_ready = sem("rows_ready")
        rows_out = sem("rows_out")
        copied = sem("copied")
        copies_done = sem("copies_done")
        norm = TokenNorm(nc, g, sem, x_in)
        block = ctx.enter_context(nc.Block())
        EXP_STEPS = [64, 32, 16, 8, 4, 2, 1]
        MANTISSA = 23

        @block.sync
        def _(sp):
            norm.load(sp)
            for dst, src in ((wr[:, :, :], w_r.rearrange("(c p) e -> p c e", p=P)), (br[:, :], b_r.partition_broadcast(P)),
                             (tri_sb[:, :], tri),
                             (segment[:, :], seg.partition_broadcast(P)), (tokp[:, :], tok_p),
                             (tokt[:, :, :].rearrange("p e t -> p (e t)"), tok_t.partition_broadcast(P))):
                sp.dma_start(dst, src).then_inc(const_in, 16)
            for to, source in copies:
                sp.dma_start(to, source).then_inc(copied, 16)
            if copies:
                sp.wait_ge(copied, 16 * len(copies))
            sp.sem_inc(copies_done, 1)
            sp.wait_ge(rows_ready, 1)
            sp.dma_start(rows_dram.rearrange("(t p) r -> p t r", p=P), g.rows[:, :, :]).then_inc(rows_out, 16)
            sp.wait_ge(rows_out, 16)

        @block.vector
        def _(dve):
            norm.statistics(dve)
            dve.wait_ge(const_in, 16 * 6)
            nc.vector.tensor_copy(tri_bf[:, :], tri_sb[:, :]).then_inc(const_ready, 1)
            nc.vector.memset(ones_bf[:, :], 1.0).then_inc(const_ready, 1)
            with dve.Fori(0, TILES // 4) as i:
                for k in range(4):
                    t = i * 4 + k
                    last = nc.vector.tensor_scalar(
                        g.rows[:, bass.ds(t, 1), 0:DIM].rearrange("p a d -> p (a d)"),
                        g.x[:, bass.ds(t, 1), :].rearrange("p a d -> p (a d)"),
                        g.aggr[:, bass.ds(t, 1), 0], g.rstd[:, bass.ds(t, 1)], ALU.subtract, ALU.mult)
                last.then_inc(xn_ready, 1)
            link = chain(dve, step_done)
            dve.wait_ge(routed, TILES // 4)
            link(nc.vector.tensor_tensor(logit[:, :, :], psR[:, :, :], br[:, :].unsqueeze(1).broadcast_to([P, TILES, EXPERTS]), ALU.add))
            link(nc.vector.tensor_reduce(top[:, :], logit[:, :, :], AX_X, ALU.max))
            nc.vector.tensor_tensor(logit[:, :, :], logit[:, :, :], top[:, :].unsqueeze(2).broadcast_to([P, TILES, EXPERTS]), ALU.subtract).then_inc(shifted, 1)
            dve.wait_ge(exp_ready, 1)
            link(nc.vector.tensor_reduce(top[:, :], logit[:, :, :], AX_X, ALU.add))
            link(nc.vector.reciprocal(top[:, :], top[:, :]))
            link(nc.vector.tensor_tensor(prob[:, :, :].rearrange("p e t -> p t e"), logit[:, :, :], top[:, :].unsqueeze(2).broadcast_to([P, TILES, EXPERTS]), ALU.mult))
            nc.vector.tensor_copy(g.rows[:, :, DIM:ROW], prob[:, :, :].rearrange("p e t -> p t e")).then_inc(rows_ready, 1)
            link(nc.vector.memset(thr[:, :], 2.0 ** -126))
            link(nc.vector.tensor_scalar(cand[:, :], thr[:, :], 2.0 ** EXP_STEPS[0], None, ALU.mult))

            def at_or_above():
                link(nc.vector.tensor_tensor(ge[:, :, :], prob[:, :, :], cand[:, :].unsqueeze(2).broadcast_to([P, EXPERTS, TILES]), ALU.is_ge))
                nc.vector.tensor_reduce(count[:, :], ge[:, :, :], AX_X, ALU.add).then_inc(counted, 1)

            def keep():
                link(nc.vector.scalar_tensor_tensor(kept[:, :], psC[:, 0:EXPERTS], float(CAPACITY), cand[:, :], ALU.is_ge, ALU.mult))
                link(nc.vector.tensor_tensor(thr[:, :], thr[:, :], kept[:, :], ALU.max))

            with nc.allow_low_precision(reason="counts of at most 32 are exact in bfloat16"):
                for k, e in enumerate(EXP_STEPS):
                    at_or_above()
                    dve.wait_ge(summed, k + 1)
                    keep()
                    if k + 1 < len(EXP_STEPS):
                        link(nc.vector.tensor_scalar(cand[:, :], thr[:, :], 2.0 ** EXP_STEPS[k + 1], None, ALU.mult))
                link(nc.vector.tensor_scalar(base[:, :], thr[:, :], 0.5, None, ALU.mult))
                for k in range(MANTISSA):
                    link(nc.vector.scalar_tensor_tensor(cand[:, :], base[:, :], 2.0 ** -k, thr[:, :], ALU.mult, ALU.add))
                    at_or_above()
                    dve.wait_ge(summed, len(EXP_STEPS) + k + 1)
                    keep()
                link(nc.vector.tensor_copy(cand[:, :], thr[:, :]))
                at_or_above()
                dve.wait_ge(summed, len(EXP_STEPS) + MANTISSA + 1)
                link(nc.vector.scalar_tensor_tensor(thr[:, :], psC[:, 0:EXPERTS], float(CAPACITY), cand[:, :], ALU.is_ge, ALU.mult))
            wide = thr[:, :].unsqueeze(2).broadcast_to([P, EXPERTS, TILES])
            nc.vector.tensor_tensor(mask[:, 0], prob[:, :, :], wide, ALU.is_gt).then_inc(masks_ready, 1)
            nc.vector.tensor_tensor(mask[:, 1], prob[:, :, :], wide, ALU.is_equal).then_inc(masks_ready, 1)
            dve.wait_ge(masks_ready, 2)
            flat = lambda a: a.rearrange("p m e t -> p (m e t)")
            dve.wait_ge(prefix_done, 1)
            link(nc.vector.tensor_copy(flat(total[:, :, :, :]), psC[:, :]))
            dve.sem_inc(total_ready, 1)
            link(nc.vector.tensor_tensor_scan(flat(running[:, :, :, :]), segment[:, :], flat(total[:, :, :, :]), 0.0, ALU.mult, ALU.add))
            link(nc.vector.tensor_tensor(flat(before[:, :, :, :]), flat(running[:, :, :, :]), flat(total[:, :, :, :]), ALU.subtract))
            dve.wait_ge(prefix_done, 2)
            link(nc.vector.tensor_tensor(flat(before[:, :, :, :]), flat(before[:, :, :, :]), psC[:, :], ALU.add))
            link(nc.vector.tensor_tensor(before[:, 1], before[:, 1], running[:, 0, :, TILES - 1:TILES].broadcast_to([P, EXPERTS, TILES]), ALU.add))
            link(nc.vector.tensor_tensor(before[:, :, :, :], before[:, :, :, :], mask[:, :, :, :], ALU.mult))
            link(nc.vector.tensor_tensor(pos[:, :, :], before[:, 0], before[:, 1], ALU.add))
            link(nc.vector.tensor_tensor(hi[:, :, :], mask[:, 0], mask[:, 1], ALU.add))
            link(nc.vector.tensor_scalar(hi[:, :, :], hi[:, :, :], -BLOCKED, BLOCKED, ALU.mult, ALU.add))
            link(nc.vector.tensor_tensor(pos[:, :, :], pos[:, :, :], hi[:, :, :], ALU.add))
            link(nc.vector.tensor_scalar(hi[:, :, :], pos[:, :, :], float(P), None, ALU.is_ge))
            for k in range(2, EC):
                link(nc.vector.scalar_tensor_tensor(hi[:, :, :], pos[:, :, :], float(k * P), hi[:, :, :], ALU.is_ge, ALU.add))
            link(nc.vector.scalar_tensor_tensor(low[:, :, :], hi[:, :, :], -float(P), pos[:, :, :], ALU.mult, ALU.add))
            for k in range(EC):
                nc.vector.tensor_scalar(values[:, :, :, k, 0], hi[:, :, :], float(k), tokp[:, 0:1], ALU.is_equal, ALU.mult)
                nc.vector.scalar_tensor_tensor(values[:, :, :, k, 1], hi[:, :, :], float(k), tokt[:, :, :], ALU.is_equal, ALU.mult)

        @block.gpsimd
        def _(pool):
            norm.roots(pool)

        @block.scalar
        def _(act):
            def copy_tokens(n):
                act.wait_ge(transposed, n + 1)
                nc.scalar.copy(xT[:, n % 2], psT[:, n % 2]).then_inc(xT_ready, 1)

            copy_tokens(0)
            for n in range(TILES // 4):
                if n + 1 < TILES // 4:
                    copy_tokens(n + 1)
                act.wait_ge(by_expert_done, n + 1)
                if n >= 2:
                    act.wait_ge(routed, n - 1)
                nc.scalar.copy(by_expert[:, n % 2], psE[0:EXPERTS, n % 2]).then_inc(by_expert_ready, 1)
            act.wait_ge(shifted, 1)
            nc.scalar.activation(logit[:, :, :], logit[:, :, :], ACT.Exp).then_inc(exp_ready, 1)

        @block.tensor
        def _(pe):
            def transposes(n, slot):
                pe.wait_ge(xn_ready, n + 1)
                for k in range(4):
                    for c in range(KC):
                        last = nc.tensor.transpose(psT[:, slot, k, c, :], g.rows[:, n * 4 + k, c * P:(c + 1) * P], g.ident[:, :])
                last.then_inc(transposed, 1)

            def to_tokens(n):
                pe.wait_ge(by_expert_ready, n + 1)
                for k in range(4):
                    last = nc.tensor.transpose(psR[:, n * 4 + k, :], by_expert[:, n % 2, k, :], g.ident[0:EXPERTS, 0:EXPERTS])
                last.then_inc(routed, 1)

            pe.wait_ge(const_ready, 2)
            pe.wait_ge(copies_done, 1)
            transposes(0, 0)
            for n in range(TILES // 4):
                slot = n % 2
                if n + 1 < TILES // 4:
                    if n >= 1:
                        pe.wait_ge(xT_ready, n)
                    transposes(n + 1, 1 - slot)
                pe.wait_ge(xT_ready, n + 1)
                if n >= 2:
                    pe.wait_ge(by_expert_ready, n - 1)
                for c in range(KC):
                    last = nc.tensor.matmul(psE[0:EXPERTS, slot], wr[:, c, :], xT[:, slot, :, c, :], start=c == 0, stop=c == KC - 1)
                last.then_inc(by_expert_done, 1)
                if n >= 1:
                    to_tokens(n - 1)
            to_tokens(TILES // 4 - 1)
            for k in range(len(EXP_STEPS) + MANTISSA + 1):
                pe.wait_ge(counted, k + 1)
                nc.tensor.matmul(psC[:, 0:EXPERTS], ones_bf[:, :], count[:, :], start=True, stop=True).then_inc(summed, 1)
            pe.wait_ge(masks_ready, 2)
            flat = mask[:, :, :, :].rearrange("p m e t -> p (m e t)")
            nc.tensor.matmul(psC[:, :], ones_bf[:, :], flat, start=True, stop=True).then_inc(prefix_done, 1)
            pe.wait_ge(total_ready, 1)
            nc.tensor.matmul(psC[:, :], tri_bf[:, :], flat, start=True, stop=True).then_inc(prefix_done, 1)


def experts(nc, g, name, x_dram, rows_dram, w_up, b_up, w_down, b_down, iota128):
    with ExitStack() as ctx:
        sb = lambda n, s, d=F32: ctx.enter_context(nc.sbuf_tensor(f"{name}_{n}", s, d))
        ps = lambda n, s: ctx.enter_context(nc.psum_tensor(f"{name}_{n}", s, F32))
        sem = ctx.enter_context(stage_semaphores(nc, name))
        rows = sb("rows", [P, EXPERTS * EC, ROW])
        rowsT = sb("rowsT", [P, KC, CAPACITY])
        wup = sb("wup", [P, KC, FFN])
        bup = sb("bup", [P, FB, EXPERTS // PER_GROUP])
        wdown = sb("wdown", [P, PER_GROUP, FB, DIM])
        bdown = sb("bdown", [P, EXPERTS, DIM])
        hidden = sb("hidden", [P, 2, FB, CAPACITY])
        y = sb("y", [P, 2, EC, DIM])
        iota_row = sb("iota_row", [P, P])
        onehot = sb("onehot", [P, 2, TILES, P], BF16)
        number = sb("number", [P, EXPERTS, EC, 2])
        index = sb("index", [P, EXPERTS, EC], I32)
        psI = ps("psI", [P, 2, 512])
        psT = ps("psT", [P, KC, CAPACITY])
        psU = ps("psU", [P, 2, CAPACITY])
        psD = ps("psD", [P, EC, DIM])

        const_in = sem("const_in")
        gathered = [sem(f"gathered{e}") for e in range(EXPERTS)]
        iota_in = sem("iota_in")
        onehot_ready = sem("onehot_ready")
        listed = sem("listed")
        number_ready = sem("number_ready")
        index_ready = sem("index_ready")
        up_in = sem("up_in")
        down_in = [sem(f"down_in{m}") for m in range(PER_GROUP)]
        transposed = sem("transposed")
        rowsT_ready = sem("rowsT_ready")
        up_done = sem("up_done")
        hidden_ready = sem("hidden_ready")
        down_done = sem("down_done")
        y_bias = sem("y_bias")
        y_ready = sem("y_ready")
        added = sem("added")
        block = ctx.enter_context(nc.Block())
        GROUPS_ = EXPERTS // PER_GROUP
        size = lambda f: P if f < FB - 1 else FLAST

        @block.sync
        def _(sp):
            full = (FB - 1) * P
            sp.dma_start(iota_row[:, :], iota128.partition_broadcast(P)).then_inc(iota_in, 16)
            sp.dma_start(bup[:, 0:FB - 1, :], b_up[0:full, :].rearrange("(f p) g -> p f g", p=P)).then_inc(const_in, 16)
            sp.dma_start(bup[0:FLAST, FB - 1, :], b_up[full:FFN, :]).then_inc(const_in, 16)
            sp.dma_start(bdown[:, :, :].rearrange("p e d -> p (e d)"), b_down.partition_broadcast(P)).then_inc(const_in, 16)
            for gr in range(GROUPS_):
                if gr:
                    sp.wait_ge(up_done, gr * PER_GROUP * FB)
                sp.dma_start(wup[:, :, :], w_up[gr].rearrange("(c p) f -> p c f", p=P)).then_inc(up_in, 16)
                for m in range(PER_GROUP):
                    e = gr * PER_GROUP + m
                    if gr:
                        sp.wait_ge(down_done, e - PER_GROUP + 1)
                    sp.dma_start(wdown[:, m, 0:FB - 1, :], w_down[e, 0:full, :].rearrange("(f p) d -> p f d", p=P)).then_inc(down_in[m], 16)
                    sp.dma_start(wdown[0:FLAST, m, FB - 1, :], w_down[e, full:FFN, :]).then_inc(down_in[m], 16)

        @block.gpsimd
        def _(pool):
            for e in range(EXPERTS):
                pool.wait_ge(index_ready, e + 1)
                for k in range(EC):
                    c = e * EC + k
                    nc.gpsimd.indirect_dma_start(
                        rows[:, c, :], None, rows_dram, bass.IndirectOffsetOnAxis(ap=index[:, e, k:k + 1], axis=0)).then_inc(gathered[e], 16)
            for e in range(EXPERTS):
                pool.wait_ge(y_ready, e + 1)
                if e:
                    pool.wait_ge(added, e * EC * 16)
                for k in range(EC):
                    c = e * EC + k
                    nc.gpsimd.indirect_dma_start(
                        x_dram, bass.IndirectOffsetOnAxis(ap=index[:, e, k:k + 1], axis=0), y[:, e % 2, k, :], None,
                        compute_op=ALU.add).then_inc(added, 16)
            pool.wait_ge(added, EXPERTS * EC * 16)

        @block.vector
        def _(dve):
            dve.wait_ge(iota_in, 16)

            def make_index(e):
                dve.wait_ge(listed, e + 1)
                nc.vector.tensor_copy(number[:, e], psI[:, e % 2, 0:EC * 2].rearrange("p (k v) -> p k v", v=2)).then_inc(number_ready, 1)
                dve.wait_ge(number_ready, e + 1)
                nc.vector.scalar_tensor_tensor(index[:, e, :], number[:, e, :, 1], float(P), number[:, e, :, 0],
                                               ALU.mult, ALU.add).then_inc(index_ready, 1)

            for e in range(EXPERTS):
                if e >= 2:
                    dve.wait_ge(listed, e - 1)
                nc.vector.tensor_tensor(onehot[:, e % 2], g.place[:, e, :].unsqueeze(2).broadcast_to([P, TILES, P]),
                                        iota_row[:, :].unsqueeze(1).broadcast_to([P, TILES, P]), ALU.is_equal).then_inc(onehot_ready, 1)
                if e == 0:
                    make_index(0)
                elif e >= 2:
                    make_index(e - 1)
            make_index(EXPERTS - 1)
            dve.wait_ge(const_in, 48)
            for e in range(EXPERTS):
                slot = e % 2
                dve.wait_ge(down_done, e + 1)
                if e >= 2:
                    dve.wait_ge(added, (e - 1) * EC * 16)
                nc.vector.tensor_tensor(y[:, slot], psD[:, :, :], bdown[:, e, :].unsqueeze(1).broadcast_to([P, EC, DIM]), ALU.add).then_inc(y_bias, 1)
                dve.wait_ge(y_bias, e + 1)
                for k in range(EC):
                    c = e * EC + k
                    last = nc.vector.tensor_scalar(y[:, slot, k, :], y[:, slot, k, :], rows[:, c, DIM + e:DIM + e + 1], 0.5, ALU.mult, ALU.mult)
                last.then_inc(y_ready, 1)

        @block.scalar
        def _(act):
            act.wait_ge(const_in, 48)
            for e in range(EXPERTS):
                act.wait_ge(transposed, e + 1)
                nc.scalar.copy(rowsT[:, :, :], psT[:, :, :]).then_inc(rowsT_ready, 1)
                for f in range(FB):
                    n = e * FB + f
                    act.wait_ge(up_done, n + 1)
                    if e >= 2 and f == 0:
                        act.wait_ge(down_done, e - 1)
                    nc.scalar.activation(hidden[0:size(f), e % 2, f, :], psU[0:size(f), n % 2, :], ACT.Silu,
                                         bias=bup[0:size(f), f, e // PER_GROUP:e // PER_GROUP + 1]).then_inc(hidden_ready, 1)

        @block.tensor
        def _(pe):
            def make_list(e):
                pe.wait_ge(onehot_ready, e + 1)
                if e >= 2:
                    pe.wait_ge(number_ready, e - 1)
                for t in range(TILES):
                    last = nc.tensor.matmul(psI[:, e % 2, 0:EC * 2], onehot[:, e % 2, t, :],
                                            g.values[:, e, t].rearrange("p k v -> p (k v)"), start=t == 0, stop=t == TILES - 1)
                last.then_inc(listed, 1)

            def take(e):
                pe.wait_ge(gathered[e], EC * 16)
                if e:
                    pe.wait_ge(rowsT_ready, e)
                for k in range(EC):
                    for c in range(KC):
                        last = nc.tensor.transpose(psT[:, c, k * P:(k + 1) * P], rows[:, e * EC + k, c * P:(c + 1) * P], g.ident[:, :])
                last.then_inc(transposed, 1)

            def up(e):
                pe.wait_ge(up_in, (e // PER_GROUP + 1) * 16)
                pe.wait_ge(rowsT_ready, e + 1)
                for f in range(FB):
                    n = e * FB + f
                    if n >= 2:
                        pe.wait_ge(hidden_ready, n - 1)
                    for c in range(KC):
                        last = nc.tensor.matmul(psU[0:size(f), n % 2, :], wup[:, c, f * P:f * P + size(f)], rowsT[:, c, :], start=c == 0, stop=c == KC - 1)
                    last.then_inc(up_done, 1)

            def down(e):
                pe.wait_ge(down_in[e % PER_GROUP], (e // PER_GROUP + 1) * 32)
                pe.wait_ge(hidden_ready, (e + 1) * FB)
                if e:
                    pe.wait_ge(y_ready, e)
                for k in range(EC):
                    for f in range(FB):
                        last = nc.tensor.matmul(psD[:, k, :], hidden[0:size(f), e % 2, f, k * P:(k + 1) * P], wdown[0:size(f), e % PER_GROUP, f, :],
                                                start=f == 0, stop=f == FB - 1)
                last.then_inc(down_done, 1)

            make_list(0)
            make_list(1)
            take(0)
            make_list(2)
            up(0)
            make_list(3)
            make_list(4)
            take(1)
            for e in range(EXPERTS):
                if e + 1 < EXPERTS:
                    up(e + 1)
                if e == 0:
                    for later in range(5, EXPERTS):
                        make_list(later)
                if e + 2 < EXPERTS:
                    take(e + 2)
                down(e)


def moe(nc, g, name, a, x_dram, x_from, rows_dram, copies=()):
    with ExitStack() as ctx:
        g.place = ctx.enter_context(nc.sbuf_tensor(f"{name}_place", [P, EXPERTS, TILES], F32))
        g.values = ctx.enter_context(nc.sbuf_tensor(f"{name}_values", [P, EXPERTS, TILES, EC, 2], BF16))
        with residual(nc, g, name), nc.sbuf_tensor(f"{name}_gather_rows", [P, TILES, ROW], F32) as g.rows:
            route(nc, g, f"{name}_r", a["Wr"], a["br"], rows_dram, a["tri"], a["seg"], a["tok_p"], a["tok_t"], x_from, copies)
        experts(nc, g, f"{name}_x", x_dram, rows_dram, a["W_up"], a["b_up"], a["W_down"], a["b_down"], a["iota"])


def program(nc, a, out):
    with ExitStack() as ctx:
        g = Common()
        g.ident = ctx.enter_context(nc.sbuf_tensor("ident", [P, P], F32))
        x_dram = nc.dram_tensor("x_scratch", [TILES * P, DIM], F32).ap()
        rows_dram = nc.dram_tensor("rows_scratch", [TILES * P, ROW], F32).ap()
        moe(nc, g, "moe1", a, x_dram, a["x"], rows_dram, ((g.ident[:, :], a["ident"]), (x_dram, a["x"])))
        talking_heads(nc, g, x_dram, a["Wqkv"], a["bqkv"], a["Wpre"], a["Wpost"], a["Wpost_all"], a["Wout"], a["bout"], a["cos"], a["sin"], a["same_token"])
        moe(nc, g, "moe2", a, x_dram, x_dram, rows_dram)
        with residual(nc, g, "last"):
            channel_mix(nc, g, "mix1", a["W_r"], a["W_k"], a["W_v"], a["mu_r"], a["mu_k"], x_dram)
            linear_attention(nc, g, "lin", a["w_qkv"], a["proj_matrix"], a["w_out"], a["b_out"])
            channel_mix(nc, g, "mix2", a["W_r"], a["W_k"], a["W_v"], a["mu_r"], a["mu_k"])
            store(nc, g, out)


def kernel(**inputs):
    import numpy as _np
    import concourse.bacc as _bacc
    from concourse import mybir as _mybir
    from concourse.bass_utils import run_bass_kernel_spmd as _run

    f32 = _np.float32
    w = {name: _np.asarray(value) for name, value in inputs.items()}
    inv = (1.0 / f32(10000.0) ** (_np.arange(0, HD, 2, dtype=f32) / f32(HD))).astype(f32)
    angle = (_np.arange(SEQ, dtype=f32)[:, None] * inv[None, :]).astype(f32).astype(_np.float64)
    arrays = {
        "x": w["L0_attn_x"].reshape(BATCH * SEQ, DIM),
        "Wqkv": w["L0_attn_Wqkv"].T,
        "bqkv": w["L0_attn_bqkv"],
        "Wpre": _np.repeat(w["L0_attn_Wpre"].T, HD, axis=0),
        "Wpost": _np.repeat(w["L0_attn_Wpost"].T, GI, axis=0),
        "Wpost_all": w["L0_attn_Wpost"].reshape(-1),
        "Wout": _np.repeat(w["L0_attn_Wout"].T.reshape(OC, HEADS // OC, 1, HD, DIM), 2, axis=2).reshape(OC, P, DIM).transpose(1, 0, 2),
        "bout": w["L0_attn_bout"],
        "cos": _np.cos(angle).astype(f32),
        "sin": _np.sin(angle).astype(f32),
        "same_token": _np.tile(_np.eye(GI, dtype=f32), (HEADS, HEADS)),
        "ident": _np.eye(P, dtype=f32),
        "Wr": w["L0_ffn_Wr"],
        "br": w["L0_ffn_br"],
        "W_up": w["L0_ffn_W_up"],
        "b_up": w["L0_ffn_b_up"].T,
        "W_down": w["L0_ffn_W_down"],
        "b_down": w["L0_ffn_b_down"].reshape(-1),
        "iota": _np.arange(P, dtype=f32),
        "tri": _np.triu(_np.ones((P, P), f32), 1),
        "seg": _np.tile((_np.arange(TILES) > 0).astype(f32), 2 * EXPERTS),
        "tok_p": _np.arange(P, dtype=f32)[:, None],
        "tok_t": _np.tile(_np.arange(TILES, dtype=f32), EXPERTS),
        "w_qkv": w["L1_attn_w_qkv"],
        "proj_matrix": w["L1_attn_proj_matrix"],
        "w_out": w["L1_attn_w_out"],
        "b_out": w["L1_attn_b_out"],
        "W_r": w["L1_ffn_W_r"].T,
        "W_k": w["L1_ffn_W_k"].T,
        "W_v": w["L1_ffn_W_v"].T,
        "mu_r": w["L1_ffn_mu_r"].reshape(KC, P).T,
        "mu_k": w["L1_ffn_mu_k"].reshape(KC, P).T,
    }
    nc = _bacc.Bacc("TRN2", target_bir_lowering=False, num_devices=1)
    feed, args = {}, {}
    for name, array in arrays.items():
        array = _np.ascontiguousarray(array)
        feed[f"in_{name}"] = array
        args[name] = nc.dram_tensor(f"in_{name}", array.shape, _mybir.dt.from_np(array.dtype), kind="ExternalInput").ap()
    out = nc.dram_tensor("out", (BATCH * SEQ, DIM), F32, kind="ExternalOutput").ap()
    program(nc, args, out)
    r = _run(nc, [feed], core_ids=[0])
    return r.results[0]["out"].reshape(BATCH, SEQ, DIM)
```
